# Optimizing a Trainium2 kernel written in Bass

```python
import numpy as np
import jax
import jax.numpy as jnp

def _softmax(x, axis=-1):
    return jax.nn.softmax(x, axis=axis)

def _gelu(x):
    return jax.nn.gelu(x, approximate=True)

def _silu(x):
    return jax.nn.silu(x)

def _sigmoid(x):
    return jax.nn.sigmoid(x)

def _layernorm(x, axis=-1, eps=1e-05):
    m = jnp.mean(x, axis=axis, keepdims=True)
    v = jnp.var(x, axis=axis, keepdims=True)
    return (x - m) / jnp.sqrt(v + eps)

def _scatter_add(tgt, idx, src, axis=0):
    return tgt.at[idx].add(src)

def _segment_sum(src, seg, n):
    return jax.ops.segment_sum(src, seg, n)
kernel_name = 'mk_dlrm_tower_d1_rec_r8_f6bb90'

def setup_inputs(seed: int=0):
    np.random.seed(seed)
    _w = jnp.asarray

    def _rec_inputs():
        import jax
        import jax.numpy as jnp
        _tk = jax.random.key(seed)
        ids = jnp.stack([jax.random.randint(jax.random.fold_in(_tk, 200 + f), (2048,), 0, v, jnp.int32) for f, v in enumerate([1000, 12500, 1000, 125000, 1250, 1000, 1000, 12500, 1000, 1000, 1250, 12500, 1000, 12500, 1000, 1250, 1000, 1000, 1250, 1000, 1000, 1000, 12500, 1000, 1250, 1000])], axis=1)
        tbl_0 = 0.05 * jax.random.normal(jax.random.fold_in(_tk, 500 + 0), (1000, 128), jnp.float32)
        tbl_1 = 0.05 * jax.random.normal(jax.random.fold_in(_tk, 500 + 1), (12500, 128), jnp.float32)
        tbl_2 = 0.05 * jax.random.normal(jax.random.fold_in(_tk, 500 + 2), (1000, 128), jnp.float32)
        tbl_3 = 0.05 * jax.random.normal(jax.random.fold_in(_tk, 500 + 3), (125000, 128), jnp.float32)
        tbl_4 = 0.05 * jax.random.normal(jax.random.fold_in(_tk, 500 + 4), (1250, 128), jnp.float32)
        tbl_5 = 0.05 * jax.random.normal(jax.random.fold_in(_tk, 500 + 5), (1000, 128), jnp.float32)
        tbl_6 = 0.05 * jax.random.normal(jax.random.fold_in(_tk, 500 + 6), (1000, 128), jnp.float32)
        tbl_7 = 0.05 * jax.random.normal(jax.random.fold_in(_tk, 500 + 7), (12500, 128), jnp.float32)
        tbl_8 = 0.05 * jax.random.normal(jax.random.fold_in(_tk, 500 + 8), (1000, 128), jnp.float32)
        tbl_9 = 0.05 * jax.random.normal(jax.random.fold_in(_tk, 500 + 9), (1000, 128), jnp.float32)
        tbl_10 = 0.05 * jax.random.normal(jax.random.fold_in(_tk, 500 + 10), (1250, 128), jnp.float32)
        tbl_11 = 0.05 * jax.random.normal(jax.random.fold_in(_tk, 500 + 11), (12500, 128), jnp.float32)
        tbl_12 = 0.05 * jax.random.normal(jax.random.fold_in(_tk, 500 + 12), (1000, 128), jnp.float32)
        tbl_13 = 0.05 * jax.random.normal(jax.random.fold_in(_tk, 500 + 13), (12500, 128), jnp.float32)
        tbl_14 = 0.05 * jax.random.normal(jax.random.fold_in(_tk, 500 + 14), (1000, 128), jnp.float32)
        tbl_15 = 0.05 * jax.random.normal(jax.random.fold_in(_tk, 500 + 15), (1250, 128), jnp.float32)
        tbl_16 = 0.05 * jax.random.normal(jax.random.fold_in(_tk, 500 + 16), (1000, 128), jnp.float32)
        tbl_17 = 0.05 * jax.random.normal(jax.random.fold_in(_tk, 500 + 17), (1000, 128), jnp.float32)
        tbl_18 = 0.05 * jax.random.normal(jax.random.fold_in(_tk, 500 + 18), (1250, 128), jnp.float32)
        tbl_19 = 0.05 * jax.random.normal(jax.random.fold_in(_tk, 500 + 19), (1000, 128), jnp.float32)
        tbl_20 = 0.05 * jax.random.normal(jax.random.fold_in(_tk, 500 + 20), (1000, 128), jnp.float32)
        tbl_21 = 0.05 * jax.random.normal(jax.random.fold_in(_tk, 500 + 21), (1000, 128), jnp.float32)
        tbl_22 = 0.05 * jax.random.normal(jax.random.fold_in(_tk, 500 + 22), (12500, 128), jnp.float32)
        tbl_23 = 0.05 * jax.random.normal(jax.random.fold_in(_tk, 500 + 23), (1000, 128), jnp.float32)
        tbl_24 = 0.05 * jax.random.normal(jax.random.fold_in(_tk, 500 + 24), (1250, 128), jnp.float32)
        tbl_25 = 0.05 * jax.random.normal(jax.random.fold_in(_tk, 500 + 25), (1000, 128), jnp.float32)
        _rk = jax.random.fold_in(_tk, 7)
        r_dense_output = -0.000520686 + 1.00062 * jax.random.normal(jax.random.fold_in(_rk, 101), (2048, 128), jnp.float32)
        W_top1 = 0.0405887 * jax.random.normal(jax.random.fold_in(_tk, 801), (607, 512), jnp.float32)
        W_top2 = 0.0441942 * jax.random.normal(jax.random.fold_in(_tk, 802), (512, 256), jnp.float32)
        W_top3 = 0.0625 * jax.random.normal(jax.random.fold_in(_tk, 803), (256, 1), jnp.float32)
        b_top1 = jnp.zeros((512,), jnp.float32)
        b_top2 = jnp.zeros((256,), jnp.float32)
        return (r_dense_output, ids, tbl_0, tbl_1, tbl_2, tbl_3, tbl_4, tbl_5, tbl_6, tbl_7, tbl_8, tbl_9, tbl_10, tbl_11, tbl_12, tbl_13, tbl_14, tbl_15, tbl_16, tbl_17, tbl_18, tbl_19, tbl_20, tbl_21, tbl_22, tbl_23, tbl_24, tbl_25, W_top1, b_top1, W_top2, b_top2, W_top3)
    r_dense_output, ids, tbl_0, tbl_1, tbl_2, tbl_3, tbl_4, tbl_5, tbl_6, tbl_7, tbl_8, tbl_9, tbl_10, tbl_11, tbl_12, tbl_13, tbl_14, tbl_15, tbl_16, tbl_17, tbl_18, tbl_19, tbl_20, tbl_21, tbl_22, tbl_23, tbl_24, tbl_25, W_top1, b_top1, W_top2, b_top2, W_top3 = _rec_inputs()

    def _L0_rec_setup():
        import jax, jax.numpy as jnp
        import numpy as np
        B, NUM_SPARSE, D = (2048, 26, 128)
        key = jax.random.key(seed)
        k1, k2 = jax.random.split(key)
        dense_output = jax.random.normal(k1, (B, D), dtype=jnp.float32)
        embeddings = jax.random.normal(k2, (B, NUM_SPARSE, D), dtype=jnp.float32)
        return {'dense_output': dense_output, 'embeddings': embeddings}
    _L0_rec_all = _L0_rec_setup()
    _L0_rec_in = {k: v for k, v in _L0_rec_all.items() if k in ()}
    del _L0_rec_all
    return {'r_dense_output': r_dense_output, 'ids': ids, 'tbl_0': tbl_0, 'tbl_1': tbl_1, 'tbl_2': tbl_2, 'tbl_3': tbl_3, 'tbl_4': tbl_4, 'tbl_5': tbl_5, 'tbl_6': tbl_6, 'tbl_7': tbl_7, 'tbl_8': tbl_8, 'tbl_9': tbl_9, 'tbl_10': tbl_10, 'tbl_11': tbl_11, 'tbl_12': tbl_12, 'tbl_13': tbl_13, 'tbl_14': tbl_14, 'tbl_15': tbl_15, 'tbl_16': tbl_16, 'tbl_17': tbl_17, 'tbl_18': tbl_18, 'tbl_19': tbl_19, 'tbl_20': tbl_20, 'tbl_21': tbl_21, 'tbl_22': tbl_22, 'tbl_23': tbl_23, 'tbl_24': tbl_24, 'tbl_25': tbl_25, 'W_top1': W_top1, 'b_top1': b_top1, 'W_top2': W_top2, 'b_top2': b_top2, 'W_top3': W_top3}

def reference(r_dense_output, ids, tbl_0, tbl_1, tbl_2, tbl_3, tbl_4, tbl_5, tbl_6, tbl_7, tbl_8, tbl_9, tbl_10, tbl_11, tbl_12, tbl_13, tbl_14, tbl_15, tbl_16, tbl_17, tbl_18, tbl_19, tbl_20, tbl_21, tbl_22, tbl_23, tbl_24, tbl_25, W_top1, b_top1, W_top2, b_top2, W_top3):
    import jax
    import jax.numpy as jnp

    def _L0_rec_ref(dense_output, embeddings):
        import jax, jax.numpy as jnp
        import numpy as np
        B, NUM_SPARSE, D = (2048, 26, 128)
        combined = jnp.concatenate([dense_output[:, None, :], embeddings], axis=1)
        interactions = jnp.einsum('bfd,bgd->bfg', combined, combined)
        F = combined.shape[1]
        iu, ju = jnp.triu_indices(F, k=1)
        interactions_flat = interactions[:, iu, ju]
        return jnp.concatenate([dense_output, interactions_flat], axis=1)
    e = jnp.stack([tbl_0[ids[:, 0]], tbl_1[ids[:, 1]], tbl_2[ids[:, 2]], tbl_3[ids[:, 3]], tbl_4[ids[:, 4]], tbl_5[ids[:, 5]], tbl_6[ids[:, 6]], tbl_7[ids[:, 7]], tbl_8[ids[:, 8]], tbl_9[ids[:, 9]], tbl_10[ids[:, 10]], tbl_11[ids[:, 11]], tbl_12[ids[:, 12]], tbl_13[ids[:, 13]], tbl_14[ids[:, 14]], tbl_15[ids[:, 15]], tbl_16[ids[:, 16]], tbl_17[ids[:, 17]], tbl_18[ids[:, 18]], tbl_19[ids[:, 19]], tbl_20[ids[:, 20]], tbl_21[ids[:, 21]], tbl_22[ids[:, 22]], tbl_23[ids[:, 23]], tbl_24[ids[:, 24]], tbl_25[ids[:, 25]]], axis=1)
    z = _L0_rec_ref(r_dense_output, e)
    z = z.reshape(z.shape[0], -1)
    h = jnp.concatenate([z, r_dense_output], axis=1)
    h = jnp.maximum(h @ W_top1 + b_top1, 0.0)
    h = jnp.maximum(h @ W_top2 + b_top2, 0.0)
    y = h @ W_top3
    return y

_drawn_inputs = setup_inputs


def setup_inputs(seed=0):
    import zlib

    import numpy as np

    out = dict(_drawn_inputs(seed))
    spreads = {'b_top1': (0.0, 0.1), 'b_top2': (0.0, 0.1)}
    factors = {}
    for name, (base, spread) in spreads.items():
        noise = np.random.default_rng([zlib.crc32(name.encode()), seed]).standard_normal(out[name].shape)
        drawn = base * np.exp(spread * noise) if base else spread * noise
        out[name] = jnp.asarray(drawn.astype(out[name].dtype))
    for name, factor in factors.items():
        out[name] = (out[name] * factor).astype(out[name].dtype)
    return out
```

```python
import concourse.bass as bass
from concourse import mybir
from contextlib import ExitStack

TILE, TILES, QUADS = 128, 2, 4
ONE_HOT = 8


def dlrm_tower_kernel(nc, dense, ids, ids_hot, tables, tables_hot, w_top1, b_top1, w_top2, b_top2, w_top3, out):
    fp32 = mybir.dt.float32
    fp32r = mybir.dt.float32r
    i32 = mybir.dt.int32
    ALU = mybir.AluOpType
    ACT = mybir.ActivationFunctionType

    P = 128
    D = dense.shape[1]
    B = dense.shape[0]
    NX = len(tables_hot)
    NGV = len(tables) + 1
    F = NGV + NX
    J, Q = QUADS, 32
    N = P * TILES
    R = TILES * Q
    U = B // N
    GROUPS = [range(g, min(g + 4, NGV)) for g in range(0, NGV, 4)]
    NG = len(GROUPS)
    QB = 16
    NP = F * (F - 1) // 2
    ZC = 3
    ZP = NP // ZC
    OFF = [f * (F - 1) - f * (f - 1) // 2 for f in range(F)]
    H1, H2 = w_top1.shape[1], w_top2.shape[1]
    M1, M2 = H1 // P, H2 // P
    V = tables_hot[0].shape[0]
    VC = 8
    VP = V // VC

    ORDER = [("T", 0), ("V", 0), ("O", 0), ("V", 1), ("O", 1), ("V", 2), ("G", (0, 0)), ("Z", 0), ("O", 2),
             ("G", (0, 1)), ("O", 3), ("L1", 0), ("T", 1), ("L1", 1), ("O", 4), ("G", (1, 0)), ("O", 5),
             ("L2", 0), ("O", 6), ("L2", 1), ("O", 7), ("G", (1, 1)), ("L3", 0)]
    assert NX % 2 == 0 and NX == 8 and TILES * NG % 2 == 0 and NP % ZC == 0 and V == VC * VP
    assert M1 == 4 and M2 == 2 and U * N == B and U > 3

    VB = 3
    VF = [range(f, min(f + 2 * VB, F - 1)) for f in range(0, F - 1, 2 * VB)]
    assert F % 2 == 1
    V_STEPS = [(0, 1), (2, 3), (4,)]
    Z0 = len(VF)
    Z_BATCHES = [(0, 1), (2,)]
    L10 = Z0 + 2
    L11, L20 = L10 + 1, L10 + 2
    L30 = L20 + 2
    NB = L30 + 1
    assert NB % 2 == 0 and Z0 == 5

    ctx = ExitStack()
    with ctx:
        def sb_(name, shape, dt=fp32):
            return ctx.enter_context(nc.sbuf_tensor(name, shape, dt))

        def sem(name):
            return ctx.enter_context(nc.semaphore(name))

        idx = [sb_(f"idx{s}", [P, NGV - 1], i32) for s in range(2)]
        emb = [sb_(f"emb{s}", [P, NGV, D]) for s in range(2)]
        embT = sb_("embT", [P, TILES, P * F + 32 - F])
        hotT = sb_("hotT", [P, NX, N])
        idx_hot = sb_("idx_hot", [P, NX, N], i32)
        row_i = sb_("row_i", [P, VC], i32)
        row = sb_("row", [P, VC])
        hot = [sb_(f"hot{s}", [VP, VC, N], fp32r) for s in range(2)]
        tab_hi = sb_("tab_hi", [VP, NX, VC, D], fp32r)
        tab_lo = sb_("tab_lo", [VP, NX, VC, D], fp32r)
        denseT = sb_("denseT", [P, J, R])
        dense_hi = sb_("dense_hi", [P, N], fp32r)
        dense_lo = sb_("dense_lo", [P, N], fp32r)
        gram = sb_("gram", [P, F, R])
        pairs = sb_("pairs", [R, J, NP])
        pairs_hi = sb_("pairs_hi", [ZP, ZC, N], fp32r)
        pairs_lo = sb_("pairs_lo", [ZP, ZC, N], fp32r)
        h1 = sb_("h1", [P, M1, N])
        stage = [h1[:, :, :].rearrange("p m n -> p (m n)"), gram[:, :, :].rearrange("p f r -> p (f r)")[:, 0:M1 * N]]
        assert VC * D <= M1 * N <= F * R
        h1_hi = sb_("h1_hi", [P, M1, N], fp32r)
        h1_lo = sb_("h1_lo", [P, M1, N], fp32r)
        h2 = sb_("h2", [P, M2, N])
        y = sb_("y", [1, N])
        wz_hi = sb_("wz_hi", [ZP, ZC, H1], fp32r)
        wz_lo = sb_("wz_lo", [ZP, ZC, H1], fp32r)
        wd = sb_("wd", [P, H1])
        wd_hi = sb_("wd_hi", [P, H1], fp32r)
        wd_lo = sb_("wd_lo", [P, H1], fp32r)
        w2_hi = sb_("w2_hi", [P, M1, H2], fp32r)
        w2_lo = sb_("w2_lo", [P, M1, H2], fp32r)
        w3 = sb_("w3", [P, M2])
        b1 = sb_("b1", [P, M1])
        b2 = sb_("b2", [P, M2])
        ident = sb_("ident", [P, P])

        def bank(name):
            return ctx.enter_context(nc.psum_tensor(name, [P, 512], fp32))

        tp = [bank(f"tp{i}") for i in range(2)]
        op = bank("op")
        ip = bank("ip")
        gp = [bank(f"gp{i}") for i in range(2)]
        wp = [bank(f"wp{i}") for i in range(2)]

        s_ident = sem("s_ident")
        s_zero = sem("s_zero")
        s_pad = sem("s_pad")
        s_rowi = sem("s_rowi")
        s_row = sem("s_row")
        s_stage = [sem(f"s_stage{s}") for s in range(2)]
        s_hi = sem("s_hi")
        s_lo = sem("s_lo")
        s_wd = sem("s_wd")
        s_small = sem("s_small")
        s_idx = [sem(f"s_idx{s}") for s in range(2)]
        s_dense = [sem(f"s_dense{s}") for s in range(2)]
        s_emb = [[sem(f"s_emb{s}_{g}") for g in range(NG)] for s in range(2)]
        s_idx_hot = sem("s_idx_hot")
        ip_full = sem("ip_full")
        hot_made = sem("hot_made")
        op_full = sem("op_full")
        op_free = sem("op_free")
        hot_moved = sem("hot_moved")
        tp_full = [sem(f"tp_full{b}") for b in range(2)]
        tp_free = [sem(f"tp_free{b}") for b in range(2)]
        gp_full = [sem(f"gp_full{b}") for b in range(2)]
        gp_free = [sem(f"gp_free{b}") for b in range(2)]
        wp_full = [sem(f"wp_full{b}") for b in range(2)]
        wp_free = [sem(f"wp_free{b}") for b in range(2)]
        dense_hi_done = sem("dense_hi_done")
        h1_half = sem("h1_half")
        dense_cut = sem("dense_cut")
        pairs_cut = sem("pairs_cut")
        h1_cut = sem("h1_cut")
        h1_done = sem("h1_done")
        s_out = sem("s_out")

        TU = TILES * NG // 2
        GU = TILES
        WU = NB // 2

        def wait(eng, semaphore, value):
            if not isinstance(value, int) or value > 0:
                eng.wait_ge(semaphore, value)

        def units(eng, unit):
            unit(0)
            with eng.Fori(1, U - 2) as u:
                unit(u)
            unit(U - 2)
            unit(U - 1)

        def before(u, a):
            return not isinstance(u, int) or 0 <= u + a < U

        def alone(u):
            return isinstance(u, int) and u == U - 1

        STAGED = NX + 4
        W_STEPS = {("V", 0): NX, ("Z", 0): NX + 1, ("L1", 0): NX + 2, ("L1", 1): NX + 3}

        def staged_in(k):
            return (k % 2, 16 * (k // 2 + 1)) if k < NX else (0, 16 * (NX // 2 + k - NX + (2 if k == NX + 3 else 1)))

        block = ctx.enter_context(nc.Block())

        @block.sync
        def _(sp):
            def load_tile(u, t):
                at = u * N + t * P
                sp.dma_start(idx[t][:, :], ids[bass.ds(at, P), :]).then_inc(s_idx[t], 16)
                sp.dma_start(emb[t][:, 0, :], dense[bass.ds(at, P), :]).then_inc(s_dense[t], 16)

            def load_idx_hot(v):
                sp.dma_start(idx_hot[:, :, :], ids_hot[bass.ds(v, 1), :].to_broadcast([P, NX * N])
                             .rearrange("p (x n) -> p x n", n=N)).then_inc(s_idx_hot, 16)

            def load_stage(k):
                s, _ = staged_in(k)
                if k < NX:
                    if k >= 2:
                        sp.wait_ge(s_lo, k - 1)
                    sp.dma_start(stage[s][0:VP, :], tables_hot[k].rearrange("(p c) d -> p (c d)", c=VC)).then_inc(s_stage[s], 16)
                    return
                sp.wait_ge(s_lo, k)
                if k == NX:
                    sp.dma_start(stage[s][0:ZP, :], w_top1[D:D + 2 * ZP, :].rearrange("(c p) n -> p c n", p=ZP)
                                 ).then_inc(s_stage[s], 16)
                elif k == NX + 1:
                    sp.dma_start(stage[s][0:ZP, 0:H1], w_top1[D + 2 * ZP:D + NP, :]).then_inc(s_stage[s], 16)
                elif k == NX + 2:
                    sp.dma_start(stage[s][:, :], w_top2.rearrange("(k p) n -> p k n", p=P)).then_inc(s_stage[s], 16)
                else:
                    sp.dma_start(stage[s][:, 0:H1], w_top1[0:D, :]).then_inc(s_stage[s], 16)
                    sp.dma_start(stage[s][:, H1:2 * H1], w_top1[D + NP:, :]).then_inc(s_stage[s], 16)

            load_tile(0, 0)
            load_idx_hot(0)
            load_tile(0, 1)
            for k in range(NX):
                load_stage(k)
            sp.dma_start(w3[:, :], w_top3).then_inc(s_small, 16)
            sp.dma_start(b1[:, :], b_top1).then_inc(s_small, 16)
            sp.dma_start(b2[:, :], b_top2).then_inc(s_small, 16)
            sp.wait_ge(hot_made, NX)
            load_idx_hot(1)
            load_stage(NX)

            def unit(u):
                if before(u, 1):
                    for t in range(TILES):
                        n = (t + 1) * NG - 1
                        sp.wait_ge(tp_full[n % 2], u * TU + n // 2 + 1)
                        load_tile(u + 1, t)
                        if not before(u, -1) and t == 0:
                            for k in range(NX + 1, STAGED):
                                load_stage(k)
                if before(u, 2):
                    sp.wait_ge(ip_full, (u + 1) * NX // 2)
                    load_idx_hot(u + 2)

            units(sp, unit)

        @block.gpsimd
        def _(pool):
            nc.gpsimd.memset(ident[:, :], 0.0).then_inc(s_zero, 1)
            nc.gpsimd.iota(row_i[:, :], [[1, VC]], base=0, channel_multiplier=VC).then_inc(s_rowi, 1)
            nc.gpsimd.memset(embT[:, :, P * F:], 0.0).then_inc(s_pad, 1)
            pool.wait_ge(s_zero, 1)
            nc.gpsimd.affine_select(out=ident[:, :], in_=ident[:, :], compare_op=ALU.not_equal, fill=1.0,
                                    base=0, pattern=[[-1, P]], channel_multiplier=1).then_inc(s_ident, 1)
            pool.wait_ge(s_rowi, 1)
            nc.gpsimd.tensor_copy(row[:, :], row_i[:, :]).then_inc(s_row, 1)

            turned = [pool.alloc_register(f"turned{b}") for b in range(2)]
            for b in range(2):
                pool.reg_mov(turned[b], 1)

            def unit(u):
                for t in range(TILES):
                    pool.wait_ge(s_idx[t], u * 16 + 16)
                    for g, vectors in enumerate(GROUPS):
                        b = (t * NG + g) % 2
                        if isinstance(u, int):
                            wait(pool, tp_full[b], (u - 1) * TU + (t * NG + g) // 2 + 1 if u else 0)
                        else:
                            pool.wait_ge(tp_full[b], turned[b])
                            pool.reg_add(turned[b], turned[b], 1)
                        for f in vectors:
                            if f:
                                nc.gpsimd.indirect_dma_start(
                                    emb[t][:, f, :], None, tables[f - 1],
                                    bass.IndirectOffsetOnAxis(ap=idx[t][:, f - 1:f], axis=0),
                                ).then_inc(s_emb[t][g], 16)

            units(pool, unit)

        def part(k):
            s = stage[staged_in(k)[0]]
            if k < NX:
                return s[0:VP, :], tab_hi[:, k, :, :], tab_lo[:, k, :, :]
            if k == NX:
                return s[0:ZP, :], wz_hi[:, 0:2, :], wz_lo[:, 0:2, :]
            if k == NX + 1:
                return s[0:ZP, 0:H1], wz_hi[:, 2, :], wz_lo[:, 2, :]
            if k == NX + 2:
                return s[:, :], w2_hi[:, :, :], w2_lo[:, :, :]
            return wd[:, :], wd_hi[:, :], wd_lo[:, :]

        def flat(ap):
            return ap if len(ap.shape) == 2 else ap.rearrange("p a b -> p (a b)")

        def embT_of(f, n, t):
            return embT[:, t, 0:P * F].rearrange("p (b f) -> p f b", f=F)[:, f:f + n, :]

        def copy_pairs(copy, b, vectors):
            for i, f in enumerate(vectors):
                lot = slice(i % 2 * R, i % 2 * R + R)
                last = copy(pairs[:, :, OFF[f]:OFF[f] + F - 1 - f],
                            wp[b][lot, i // 2 * P:(i // 2 + 1) * P].rearrange("p (j f) -> p j f", f=32)[:, :, f + 1:F])
            return last

        @block.vector
        def _(dve):
            def make_hot(v, k):
                n = v * NX + k
                wait(dve, op_full, n - 1)
                if isinstance(v, int) and v == 0:
                    for c in range(VC):
                        last = nc.vector.tensor_scalar(hot[k % 2][:, c, :], idx_hot[0:VP, k, :], row[0:VP, c:c + 1],
                                                       None, ALU.is_equal)
                    last.then_inc(hot_made, 1)
                    return
                if k % 2 == 0:
                    dve.wait_ge(ip_full, (v - 1) * NX // 2 + k // 2 + 1)
                indices = ip[0:VP, k % 2 * N:(k % 2 + 1) * N]
                nc.vector.tensor_tensor(hot[k % 2][:, :, :], indices.unsqueeze(1).broadcast_to([VP, VC, N]),
                                        row[0:VP, :].unsqueeze(2).broadcast_to([VP, VC, N]),
                                        ALU.is_equal).then_inc(hot_made, 1)

            def cut(k):
                src, hi, lo = part(k)
                if k == STAGED - 1:
                    place, come = staged_in(k)
                    dve.wait_ge(s_stage[place], come)
                    s = stage[place]
                    nc.vector.tensor_tensor(wd[:, :], s[:, 0:H1], s[:, H1:2 * H1], ALU.add).then_inc(s_wd, 1)
                dve.wait_ge(s_hi, k + 1)
                nc.vector.tensor_tensor(flat(lo), flat(src), flat(hi).bitcast(fp32), ALU.subtract).then_inc(s_lo, 1)

            dve.wait_ge(s_row, 1)
            dve.wait_ge(s_idx_hot, 16)
            for k in range(NX):
                make_hot(0, k)
                cut(k)
            make_hot(1, 0)
            make_hot(1, 1)

            def unit(u):
                dve.wait_ge(op_free, (u + 1) * NX)
                if before(u, -1):
                    dve.wait_ge(gp_full[1], u * GU)
                for t in range(TILES):
                    nc.vector.tensor_copy(embT_of(NGV, NX, t), hotT[:, :, t * P:(t + 1) * P]).then_inc(hot_moved, 1)
                for step, a in ORDER:
                    if step == "O" and a == 4:
                        if before(u, -1):
                            dve.wait_ge(wp_full[L11 % 2], (u - 1) * WU + L11 // 2 + 1)
                        cut_dense(u)
                    if step == "O" and before(u, 1):
                        if a + 2 < NX:
                            make_hot(u + 1, a + 2)
                        elif before(u, 2):
                            make_hot(u + 2, a + 2 - NX)
                    elif before(u, -1):
                        tower(u - 1, step, a)
                    elif (step, a) in W_STEPS:
                        cut(W_STEPS[step, a])

            def cut_dense(u):
                for b in range(2):
                    dve.wait_ge(tp_free[b], (u + 1) * TU)
                src = denseT[:, :, :].rearrange("p j r -> p (j r)")
                nc.vector.tensor_copy(dense_hi[:, :], src).then_inc(dense_hi_done, 1)
                dve.wait_ge(dense_hi_done, u + 1)
                nc.vector.tensor_tensor(dense_lo[:, :], src, dense_hi[:, :].bitcast(fp32), ALU.subtract).then_inc(dense_cut, 1)

            def tower(u, step, a):
                if step == "V":
                    for i in V_STEPS[a]:
                        if alone(u) and i % 2 == 0:
                            dve.wait_ge(wp_full[0], u * WU + i // 2 + 1)
                            copy_pairs(nc.vector.tensor_copy, 0, VF[i]).then_inc(wp_free[0], 1)
                elif step == "Z":
                    for i, chunks in enumerate(Z_BATCHES):
                        b = (Z0 + i) % 2
                        cs = slice(chunks[0], chunks[-1] + 1)
                        dve.wait_ge(pairs_cut, u * 2 + i + 1)
                        nc.vector.tensor_tensor(flat(pairs_lo[:, cs, :]), wp[b][0:ZP, 0:len(chunks) * N],
                                                flat(pairs_hi[:, cs, :]).bitcast(fp32),
                                                ALU.subtract).then_inc(wp_free[b], 1)
                elif step == "L1":
                    dve.wait_ge(h1_cut, u * 2 + a + 1)
                    half = slice(2 * a, 2 * a + 2)
                    nc.vector.tensor_tensor(flat(h1_lo[:, half, :]), flat(h1[:, half, :]),
                                            flat(h1_hi[:, half, :]).bitcast(fp32), ALU.subtract).then_inc(h1_done, 1)

            units(dve, unit)
            for step, a in ORDER:
                if step in ("V", "Z", "L1"):
                    tower(U - 1, step, a)

        @block.scalar
        def _(act):
            def copy(dst, src):
                return nc.scalar.activation(dst, src, ACT.Copy)

            def indices(v, k):
                n = v * NX + k
                act.wait_ge(hot_made, n)
                if k == 0:
                    act.wait_ge(s_idx_hot, v * 16 + 16)
                copy(ip[0:VP, :], flat(idx_hot[0:VP, k:k + 2, :])).then_inc(ip_full, 1)

            def cut(k):
                src, hi, _ = part(k)
                if k < STAGED - 1:
                    place, come = staged_in(k)
                    act.wait_ge(s_stage[place], come)
                else:
                    act.wait_ge(s_wd, 1)
                copy(flat(hi), src).then_inc(s_hi, 1)

            def looked_up(v, k):
                n = v * NX + k
                act.wait_ge(op_full, n + 1)
                copy(hotT[:, k, :], op[:, 0:N]).then_inc(op_free, 1)

            for k in range(NX):
                cut(k)
                if k:
                    looked_up(0, k - 1)
            looked_up(0, NX - 1)
            indices(1, 0)
            act.wait_ge(s_small, 48)

            def unit(u):
                wait(act, dense_cut, u)
                for step, a in ORDER:
                    if step == "O" and a == 0:
                        act.wait_ge(hot_moved, (u + 1) * TILES)
                    if step == "T":
                        for g, vectors in enumerate(GROUPS):
                            n = a * NG + g
                            b = n % 2
                            act.wait_ge(tp_full[b], u * TU + n // 2 + 1)
                            if g == 0:
                                copy(denseT[:, :, a * Q:(a + 1) * Q],
                                     tp[b][:, 0:P].rearrange("p (j q) -> p j q", q=Q))
                            copy(embT_of(vectors[0], len(vectors), a),
                                 tp[b][:, 0:len(vectors) * P].rearrange("p (f b) -> p f b", b=P)
                                 ).then_inc(tp_free[b], 1)
                    elif step == "G":
                        t, b = a
                        act.wait_ge(gp_full[b], u * GU + t + 1)
                        at = t * Q + b * QB
                        copy(gram[:, :, at:at + QB].rearrange("p f r -> p r f"),
                             gp[b][:, 0:QB * F].rearrange("p (q f) -> p q f", f=F)).then_inc(gp_free[b], 1)
                    elif step == "O":
                        if before(u, 1):
                            looked_up(u + 1, a)
                            if a % 2 == 0:
                                if a + 2 < NX:
                                    indices(u + 1, a + 2)
                                elif before(u, 2):
                                    indices(u + 2, 0)
                    elif before(u, -1):
                        tower(u - 1, step, a)
                    elif (step, a) in W_STEPS:
                        cut(W_STEPS[step, a])

            def tower(u, step, a):
                if step == "V":
                    for i in V_STEPS[a]:
                        b = i % 2
                        if b == 1 or not alone(u):
                            act.wait_ge(wp_full[b], u * WU + i // 2 + 1)
                            copy_pairs(copy, b, VF[i]).then_inc(wp_free[b], 1)
                elif step == "Z":
                    for i, chunks in enumerate(Z_BATCHES):
                        n = Z0 + i
                        act.wait_ge(wp_full[n % 2], u * WU + n // 2 + 1)
                        copy(flat(pairs_hi[:, chunks[0]:chunks[-1] + 1, :]),
                             wp[n % 2][0:ZP, 0:len(chunks) * N]).then_inc(pairs_cut, 1)
                elif step == "L1":
                    n = L10 + a
                    act.wait_ge(wp_full[n % 2], u * WU + n // 2 + 1)
                    for i in range(2):
                        m = 2 * a + i
                        last = nc.scalar.activation(h1[:, m, :], wp[n % 2][:, i * N:(i + 1) * N], ACT.Relu, bias=b1[:, m:m + 1])
                        last.then_inc([h1_half, wp_free[n % 2]][i], 1)
                    act.wait_ge(h1_half, u * 2 + a + 1)
                    act.wait_ge(wp_free[n % 2], u * WU + n // 2 + 1)
                    half = slice(2 * a, 2 * a + 2)
                    copy(flat(h1_hi[:, half, :]), flat(h1[:, half, :])).then_inc(h1_cut, 1)
                elif step == "L2":
                    n = L20 + a
                    act.wait_ge(wp_full[n % 2], u * WU + n // 2 + 1)
                    nc.scalar.activation(h2[:, a, :], wp[n % 2][:, 0:N], ACT.Relu, bias=b2[:, a:a + 1]).then_inc(wp_free[n % 2], 1)
                elif step == "L3":
                    n = L30
                    act.wait_ge(wp_full[n % 2], u * WU + n // 2 + 1)
                    wait(act, s_out, u * 16)
                    copy(y[:, :], wp[n % 2][0:1, 0:N]).then_inc(wp_free[n % 2], 1)
                    act.wait_ge(wp_free[n % 2], u * WU + n // 2 + 1)
                    act.dma_start(out[bass.ds(u * N, N), :].rearrange("n o -> o n"), y[:, :]).then_inc(s_out, 16)

            act.wait_ge(s_lo, NX)
            units(act, unit)
            for step, a in ORDER:
                if step in ("V", "Z", "L1", "L2", "L3"):
                    tower(U - 1, step, a)
            act.wait_ge(s_out, U * 16)

        @block.tensor
        def _(pe):
            def look_up(v, k):
                n = v * NX + k
                pe.wait_ge(hot_made, n + 1)
                wait(pe, op_free, n)
                if isinstance(v, int) and v == 0:
                    pe.wait_ge(s_lo, k + 1)
                for c in range(VC):
                    for part_of in (tab_hi, tab_lo):
                        last = nc.tensor.matmul(op[:, 0:N], part_of[:, k, c, :], hot[k % 2][:, c, :],
                                                start=(c == 0 and part_of is tab_hi),
                                                stop=(c == VC - 1 and part_of is tab_lo))
                last.then_inc(op_full, 1)

            def products(o, terms):
                all_ = [m for w_hi, w_lo, x_hi, x_lo in terms for m in ((w_hi, x_hi), (w_hi, x_lo), (w_lo, x_hi))]
                for i, (w, x) in enumerate(all_):
                    last = nc.tensor.matmul(o, w, x, start=(i == 0), stop=(i == len(all_) - 1))
                return last

            for k in range(NX):
                look_up(0, k)
            pe.wait_ge(s_ident, 1)
            pe.wait_ge(s_pad, 1)

            def unit(u):
                for step, a in ORDER:
                    if step == "T":
                        for g, vectors in enumerate(GROUPS):
                            n = a * NG + g
                            b = n % 2
                            if g == 0:
                                pe.wait_ge(s_dense[a], u * 16 + 16)
                            rows = 16 * len([f for f in vectors if f])
                            pe.wait_ge(s_emb[a][g], u * rows + rows)
                            wait(pe, tp_free[b], u * TU + n // 2)
                            for i, f in enumerate(vectors):
                                last = nc.tensor.transpose(tp[b][:, i * P:(i + 1) * P], emb[a][:, f, :], ident[:, :])
                            last.then_inc(tp_full[b], 1)
                    elif step == "G":
                        t, b = a
                        if b == 0:
                            for i in range(2):
                                pe.wait_ge(tp_free[i], u * TU + ((t + 1) * NG + 1 - i) // 2)
                            pe.wait_ge(hot_moved, u * TILES + t + 1)
                        wait(pe, gp_free[b], u * GU + t)
                        for j in range(J):
                            for q in range(QB):
                                at = (j * Q + b * QB + q) * F
                                last = nc.tensor.matmul(gp[b][32 * j:32 * j + 32, q * F:(q + 1) * F],
                                                        embT[:, t, at:at + 32], embT[:, t, at:at + F],
                                                        start=True, stop=True)
                        last.then_inc(gp_full[b], 1)
                    elif step == "O":
                        if before(u, 1):
                            look_up(u + 1, a)
                    elif before(u, -1):
                        tower(u - 1, step, a)

            turned = pe.alloc_register("turned")
            pe.reg_mov(turned, (Z0 + 1) // 2)

            def tower(u, step, a):
                if step == "V":
                    if a == 0:
                        for b in range(2):
                            pe.wait_ge(gp_free[b], (u + 1) * GU)
                    for i in V_STEPS[a]:
                        b = i % 2
                        wait(pe, wp_free[b], u * WU + i // 2)
                        for k, f in enumerate(VF[i][::2]):
                            last = nc.tensor.transpose(wp[b][:, k * P:(k + 1) * P],
                                                       gram[:, f:f + 2, :].rearrange("p f r -> p (f r)"), ident[:, :])
                        last.then_inc(wp_full[b], 1)
                elif step == "Z":
                    pe.wait_ge(wp_free[1], u * WU + Z0 // 2)
                    if isinstance(u, int):
                        pe.wait_ge(wp_free[0], u * WU + (Z0 + 1) // 2)
                    else:
                        pe.wait_ge(wp_free[0], turned)
                        pe.reg_add(turned, turned, WU)
                    for i, chunks in enumerate(Z_BATCHES):
                        b = (Z0 + i) % 2
                        for k, c in enumerate(chunks):
                            for j in range(J):
                                last = nc.tensor.transpose(wp[b][0:ZP, k * N + j * R:k * N + (j + 1) * R],
                                                           pairs[:, j, c * ZP:(c + 1) * ZP], ident[0:R, 0:R])
                        last.then_inc(wp_full[b], 1)
                elif step == "L1":
                    n = L10 + a
                    if a == 0:
                        pe.wait_ge(s_lo, STAGED)
                        for b in range(2):
                            pe.wait_ge(wp_free[b], u * WU + (L10 + 1 - b) // 2)
                        pe.wait_ge(dense_cut, u + 1)
                    wait(pe, wp_free[n % 2], u * WU + n // 2)
                    for i in range(2):
                        cols = slice((2 * a + i) * P, (2 * a + i + 1) * P)
                        last = products(wp[n % 2][:, i * N:(i + 1) * N],
                                        [(wd_hi[:, cols], wd_lo[:, cols], dense_hi[:, :], dense_lo[:, :])]
                                        + [(wz_hi[:, c, cols], wz_lo[:, c, cols], pairs_hi[:, c, :], pairs_lo[:, c, :])
                                           for c in range(ZC)])
                    last.then_inc(wp_full[n % 2], 1)
                elif step == "L2":
                    n = L20 + a
                    pe.wait_ge(h1_done, u * 2 + 2)
                    wait(pe, wp_free[n % 2], u * WU + n // 2)
                    cols = slice(a * P, (a + 1) * P)
                    products(wp[n % 2][:, 0:N], [(w2_hi[:, k, cols], w2_lo[:, k, cols], h1_hi[:, k, :], h1_lo[:, k, :])
                                                 for k in range(M1)]).then_inc(wp_full[n % 2], 1)
                elif step == "L3":
                    n = L30
                    for b in range(2):
                        pe.wait_ge(wp_free[b], u * WU + (L30 + 1 - b) // 2)
                    for k in range(M2):
                        last = nc.tensor.matmul(wp[n % 2][0:1, 0:N], w3[:, k:k + 1], h2[:, k, :],
                                                start=(k == 0), stop=(k == M2 - 1))
                    last.then_inc(wp_full[n % 2], 1)

            units(pe, unit)
            for step, a in ORDER:
                if step in ("V", "Z", "L1", "L2", "L3"):
                    tower(U - 1, step, a)


def in_tiles(a):
    q = TILE // QUADS
    a = a.reshape(a.shape[0] // (TILE * TILES), QUADS, TILES, q, a.shape[1])
    return a.transpose(0, 2, 1, 3, 4).reshape(-1, a.shape[4])


def kernel(**inputs):
    import numpy as np
    import concourse.bacc as bacc
    from concourse.bass_utils import run_bass_kernel_spmd

    nc = bacc.Bacc("TRN2", target_bir_lowering=False, num_devices=1)
    arrays = {}

    def feed(name, a):
        a = np.ascontiguousarray(a)
        arrays[f"in_{name}"] = a
        return nc.dram_tensor(f"in_{name}", a.shape, mybir.dt.from_np(a.dtype), kind="ExternalInput").ap()

    n_tables = inputs["ids"].shape[1]
    by_size = sorted(range(n_tables), key=lambda i: inputs[f"tbl_{i}"].shape[0])
    one_hot = sorted(by_size[:ONE_HOT])
    gathered = [i for i in range(n_tables) if i not in one_hot]
    order = [0] + [i + 1 for i in gathered + one_hot]

    n_vectors, width = n_tables + 1, inputs["r_dense_output"].shape[1]
    row_of, row = {}, width
    for f in range(n_vectors):
        for g in range(f + 1, n_vectors):
            row_of[f, g] = row
            row += 1
    pair_rows = [row_of[min(order[a], order[b]), max(order[a], order[b])]
                 for a in range(n_vectors) for b in range(a + 1, n_vectors)]
    w_top1 = np.asarray(inputs["W_top1"])
    w_top1 = w_top1[list(range(width)) + pair_rows + list(range(row, w_top1.shape[0]))]

    ids_rows = in_tiles(np.asarray(inputs["ids"]))
    unit = TILE * TILES
    ids_hot = ids_rows[:, one_hot].reshape(-1, unit, ONE_HOT).transpose(0, 2, 1).reshape(-1, ONE_HOT * unit)
    by_partition = [np.asarray(inputs[n]).reshape(-1, TILE).T for n in ("b_top1", "b_top2", "W_top3")]

    dense = feed("dense", in_tiles(np.asarray(inputs["r_dense_output"])))
    ids = feed("ids", ids_rows[:, gathered])
    hot = feed("ids_hot", ids_hot)
    tables = [feed(f"tbl_{i}", np.asarray(inputs[f"tbl_{i}"])) for i in gathered]
    tables_hot = [feed(f"tbl_{i}", np.asarray(inputs[f"tbl_{i}"])) for i in one_hot]
    w1 = feed("W_top1", w_top1)
    w2 = feed("W_top2", np.asarray(inputs["W_top2"]))
    b1, b2, w3 = (feed(n, a) for n, a in zip(("b_top1", "b_top2", "W_top3"), by_partition))
    out = nc.dram_tensor("out_y", (dense.shape[0], 1), mybir.dt.float32, kind="ExternalOutput").ap()
    dlrm_tower_kernel(nc, dense, ids, hot, tables, tables_hot, w1, b1, w2, b2, w3, out)
    r = run_bass_kernel_spmd(nc, [arrays], core_ids=[0])
    return r.results[0]["out_y"]
```

```python
import concourse.bass as bass
from concourse import mybir
from contextlib import ExitStack

TILE, TILES, QUADS = 128, 2, 4
ONE_HOT = 8


def dlrm_tower_kernel(nc, dense, ids, ids_hot, tables, tables_hot, w_top1, b_top1, w_top2, b_top2, w_top3, out):
    fp32 = mybir.dt.float32
    fp32r = mybir.dt.float32r
    i32 = mybir.dt.int32
    ALU = mybir.AluOpType
    ACT = mybir.ActivationFunctionType

    P = 128
    D = dense.shape[1]
    B = dense.shape[0]
    NX = len(tables_hot)
    NGV = len(tables) + 1
    F = NGV + NX
    J, Q = QUADS, 32
    N = P * TILES
    R = TILES * Q
    U = B // N
    GROUPS = [range(g, min(g + 4, NGV)) for g in range(0, NGV, 4)]
    NG = len(GROUPS)
    QB = 16
    NP = F * (F - 1) // 2
    ZC = 3
    ZP = NP // ZC
    OFF = [f * (F - 1) - f * (f - 1) // 2 for f in range(F)]
    H1, H2 = w_top1.shape[1], w_top2.shape[1]
    M1, M2 = H1 // P, H2 // P
    V = tables_hot[0].shape[0]
    VC = 8
    VP = V // VC

    T_STEPS = [(0, 1), (2, 3), (4,)]
    ORDER = [("V", 0), ("O", 0), ("V", 1), ("O", 1), ("V", 2), ("G", (0, 0)), ("Z", 0), ("O", 2), ("G", (0, 1)),
             ("T", (1, 0)), ("L1", 0), ("T", (1, 1)), ("O", 3), ("T", (1, 2)), ("L1", 1), ("O", 4), ("D", 0),
             ("G", (1, 0)), ("L2", 0), ("O", 5), ("L2", 1), ("T", (0, 0)), ("O", 6), ("T", (0, 1)), ("G", (1, 1)),
             ("O", 7), ("L3", 0), ("T", (0, 2))]
    FIRST = [("O", 0), ("G", (0, 0)), ("W", 0), ("G", (0, 1)), ("T", (1, 0)), ("O", 1), ("T", (1, 1)), ("O", 2), ("W", 1),
             ("O", 3), ("T", (1, 2)), ("G", (1, 0)), ("W", 2), ("O", 4), ("D", 0), ("W", 3), ("G", (1, 1)), ("O", 5),
             ("T", (0, 0)), ("O", 6), ("T", (0, 1)), ("O", 7), ("T", (0, 2))]
    LAST = [("V", 0), ("T", (1, 0)), ("V", 1), ("V", 2), ("G", (0, 0)), ("Z", 0), ("G", (0, 1)), ("L1", 0), ("L1", 1),
            ("D", 0), ("T", (1, 1)), ("L2", 0), ("L2", 1), ("T", (1, 2)), ("G", (1, 0)), ("L3", 0), ("G", (1, 1))]
    T_FIRST = [3, 5, 6]
    assert NX % 2 == 0 and NX == 8 and TILES * NG % 2 == 0 and NP % ZC == 0 and V == VC * VP
    assert M1 == 4 and M2 == 2 and U * N == B and U > 3

    VB = 3
    VF = [range(f, min(f + 2 * VB, F - 1)) for f in range(0, F - 1, 2 * VB)]
    assert F % 2 == 1
    V_STEPS = [(0, 1), (2, 3), (4,)]
    Z0 = len(VF)
    Z_BATCHES = [(0, 1), (2,)]
    L10 = Z0 + 2
    L11, L20 = L10 + 1, L10 + 2
    L30 = L20 + 2
    NB = L30 + 1
    LAST_V = [range(0, 6), range(6, 12), range(12, 18), range(18, F - 1)]
    LAST_SHARE = [(0, 2), (1, 3)]
    assert NB % 2 == 0 and Z0 == 5
    LAST_Z_AFTER = [(1, 0), (1, 1), (2, 2)]
    assert OFF[LAST_V[1][0]] >= ZP and OFF[LAST_V[2][0]] >= 2 * ZP

    ctx = ExitStack()
    with ctx:
        def sb_(name, shape, dt=fp32):
            return ctx.enter_context(nc.sbuf_tensor(name, shape, dt))

        def sem(name):
            return ctx.enter_context(nc.semaphore(name))

        idx = [sb_(f"idx{s}", [P, NGV - 1], i32) for s in range(2)]
        emb = [sb_(f"emb{s}", [P, NGV, D]) for s in range(2)]
        embT = sb_("embT", [P, TILES, P * F + 32 - F])
        hotT = sb_("hotT", [P, NX, N])
        idx_hot = sb_("idx_hot", [P, NX, N], i32)
        row_i = sb_("row_i", [P, VC], i32)
        row = sb_("row", [P, VC])
        hot = [sb_(f"hot{s}", [VP, VC, N], fp32r) for s in range(2)]
        tab_hi = sb_("tab_hi", [VP, NX, VC, D], fp32r)
        tab_lo = sb_("tab_lo", [VP, NX, VC, D], fp32r)
        denseT = sb_("denseT", [P, J, R])
        dense_hi = sb_("dense_hi", [P, N], fp32r)
        dense_lo = sb_("dense_lo", [P, N], fp32r)
        gram = sb_("gram", [P, F, R])
        pairs = sb_("pairs", [R, J, NP])
        pairs_hi = sb_("pairs_hi", [ZP, ZC, N], fp32r)
        pairs_lo = sb_("pairs_lo", [ZP, ZC, N], fp32r)
        h1 = sb_("h1", [P, M1, N])
        stage = [h1[:, :, :].rearrange("p m n -> p (m n)"), gram[:, :, :].rearrange("p f r -> p (f r)")[:, 0:M1 * N]]
        assert VC * D <= M1 * N <= F * R
        h1_hi = sb_("h1_hi", [P, M1, N], fp32r)
        h1_lo = sb_("h1_lo", [P, M1, N], fp32r)
        h2 = sb_("h2", [P, M2, N])
        y = sb_("y", [1, N])
        wz_hi = sb_("wz_hi", [ZP, ZC, H1], fp32r)
        wz_lo = sb_("wz_lo", [ZP, ZC, H1], fp32r)
        wd = sb_("wd", [P, H1])
        wd_hi = sb_("wd_hi", [P, H1], fp32r)
        wd_lo = sb_("wd_lo", [P, H1], fp32r)
        w2_hi = sb_("w2_hi", [P, M1, H2], fp32r)
        w2_lo = sb_("w2_lo", [P, M1, H2], fp32r)
        w3 = sb_("w3", [P, M2])
        b1 = sb_("b1", [P, M1])
        b2 = sb_("b2", [P, M2])
        ident = sb_("ident", [P, P])

        def bank(name):
            return ctx.enter_context(nc.psum_tensor(name, [P, 512], fp32))

        tp = [bank(f"tp{i}") for i in range(2)]
        op = bank("op")
        ip = bank("ip")
        gp = [bank(f"gp{i}") for i in range(2)]
        wp = [bank(f"wp{i}") for i in range(2)]

        s_ident = sem("s_ident")
        s_zero = sem("s_zero")
        s_pad = sem("s_pad")
        s_rowi = sem("s_rowi")
        s_row = sem("s_row")
        s_stage = [sem(f"s_stage{s}") for s in range(2)]
        s_hi = sem("s_hi")
        s_lo = sem("s_lo")
        s_wd = sem("s_wd")
        s_small = sem("s_small")
        s_idx = [sem(f"s_idx{s}") for s in range(2)]
        s_dense = [sem(f"s_dense{s}") for s in range(2)]
        s_emb = [[sem(f"s_emb{s}_{g}") for g in range(NG)] for s in range(2)]
        s_idx_hot = [sem(f"s_idx_hot{i}") for i in range(NX // 2)]
        ip_full = sem("ip_full")
        hot_made = sem("hot_made")
        op_full = sem("op_full")
        op_free = sem("op_free")
        hot_moved = sem("hot_moved")
        tp_full = [sem(f"tp_full{b}") for b in range(2)]
        tp_free = [sem(f"tp_free{b}") for b in range(2)]
        gp_full = [sem(f"gp_full{b}") for b in range(2)]
        gp_free = [sem(f"gp_free{b}") for b in range(2)]
        wp_full = [sem(f"wp_full{b}") for b in range(2)]
        wp_free = [sem(f"wp_free{b}") for b in range(2)]
        dense_hi_done = sem("dense_hi_done")
        h1_half = sem("h1_half")
        dense_cut = sem("dense_cut")
        pairs_cut = sem("pairs_cut")
        h1_cut = sem("h1_cut")
        h1_done = sem("h1_done")
        s_out = sem("s_out")
        v_full = sem("v_full")
        v_act = sem("v_act")
        v_dve = sem("v_dve")
        z_full = sem("z_full")
        z_hi = sem("z_hi")
        z_lo = sem("z_lo")
        l1_full = sem("l1_full")
        l1_raw = sem("l1_raw")
        l1_hi = sem("l1_hi")
        l1_lo = sem("l1_lo")
        l2_full = sem("l2_full")
        h2_act = sem("h2_act")
        h2_dve = sem("h2_dve")
        l3_full = sem("l3_full")
        y_done = sem("y_done")

        TU = TILES * NG // 2
        GU = TILES
        WU = NB // 2

        def wait(eng, semaphore, value):
            if not isinstance(value, int) or value > 0:
                eng.wait_ge(semaphore, value)

        def units(eng, unit):
            unit(0)
            with eng.Fori(1, U - 2) as u:
                unit(u)
            unit(U - 2)
            unit(U - 1)

        def before(u, a):
            return not isinstance(u, int) or 0 <= u + a < U

        def steps(u):
            return FIRST if not before(u, -1) else ORDER if before(u, 1) else LAST

        STAGED = NX + 4

        def staged_in(k):
            return (k % 2, 16 * (k // 2 + 1)) if k < NX else (0, 16 * (NX // 2 + k - NX + (2 if k == NX + 3 else 1)))

        block = ctx.enter_context(nc.Block())

        @block.sync
        def _(sp):
            def load_tile(u, t):
                at = u * N + t * P
                sp.dma_start(idx[t][:, :], ids[bass.ds(at, P), :]).then_inc(s_idx[t], 16)
                sp.dma_start(emb[t][:, 0, :], dense[bass.ds(at, P), :]).then_inc(s_dense[t], 16)

            def load_idx_hot(v, i):
                sp.dma_start(idx_hot[:, 2 * i:2 * i + 2, :],
                             ids_hot[bass.ds(v, 1), 2 * i * N:2 * (i + 1) * N].to_broadcast([P, 2 * N])
                             .rearrange("p (x n) -> p x n", n=N)).then_inc(s_idx_hot[i], 16)

            def load_stage(k):
                s, _ = staged_in(k)
                if k < NX:
                    if k >= 2:
                        sp.wait_ge(s_lo, k - 1)
                    sp.dma_start(stage[s][0:VP, :], tables_hot[k].rearrange("(p c) d -> p (c d)", c=VC)).then_inc(s_stage[s], 16)
                    return
                sp.wait_ge(s_lo, k)
                if k == NX:
                    sp.dma_start(stage[s][0:ZP, :], w_top1[D:D + 2 * ZP, :].rearrange("(c p) n -> p c n", p=ZP)
                                 ).then_inc(s_stage[s], 16)
                elif k == NX + 1:
                    sp.dma_start(stage[s][0:ZP, 0:H1], w_top1[D + 2 * ZP:D + NP, :]).then_inc(s_stage[s], 16)
                elif k == NX + 2:
                    sp.dma_start(stage[s][:, :], w_top2.rearrange("(k p) n -> p k n", p=P)).then_inc(s_stage[s], 16)
                else:
                    sp.dma_start(stage[s][:, 0:H1], w_top1[0:D, :]).then_inc(s_stage[s], 16)
                    sp.dma_start(stage[s][:, H1:2 * H1], w_top1[D + NP:, :]).then_inc(s_stage[s], 16)

            load_tile(0, 0)
            load_idx_hot(0, 0)
            load_stage(0)
            load_stage(1)
            load_idx_hot(0, 1)
            load_tile(0, 1)
            for i in range(2, NX // 2):
                load_idx_hot(0, i)
            for k in range(2, NX):
                load_stage(k)
                if k % 2:
                    i = k // 2 - 1
                    sp.wait_ge(hot_made, 2 * i + 2)
                    load_idx_hot(1, i)
            sp.dma_start(w3[:, :], w_top3).then_inc(s_small, 16)
            sp.dma_start(b1[:, :], b_top1).then_inc(s_small, 16)
            sp.dma_start(b2[:, :], b_top2).then_inc(s_small, 16)
            load_stage(NX)
            sp.wait_ge(hot_made, NX)
            load_idx_hot(1, NX // 2 - 1)

            def unit(u):
                if before(u, 1):
                    for t in range(TILES):
                        n = (t + 1) * NG - 1
                        sp.wait_ge(tp_full[n % 2], u * TU + n // 2 + 1)
                        load_tile(u + 1, t)
                        if before(u, 2):
                            for i in (2 * t, 2 * t + 1):
                                sp.wait_ge(ip_full, u * NX // 2 + i + 1)
                                load_idx_hot(u + 2, i)
                        if not before(u, -1):
                            for k in (NX + 1, NX + 2) if t == 0 else (NX + 3,):
                                load_stage(k)

            units(sp, unit)

        @block.gpsimd
        def _(pool):
            nc.gpsimd.memset(ident[:, :], 0.0).then_inc(s_zero, 1)
            nc.gpsimd.iota(row_i[:, :], [[1, VC]], base=0, channel_multiplier=VC).then_inc(s_rowi, 1)
            nc.gpsimd.memset(embT[:, :, P * F:], 0.0).then_inc(s_pad, 1)
            pool.wait_ge(s_zero, 1)
            nc.gpsimd.affine_select(out=ident[:, :], in_=ident[:, :], compare_op=ALU.not_equal, fill=1.0,
                                    base=0, pattern=[[-1, P]], channel_multiplier=1).then_inc(s_ident, 1)
            pool.wait_ge(s_rowi, 1)
            nc.gpsimd.tensor_copy(row[:, :], row_i[:, :]).then_inc(s_row, 1)

            turned = [pool.alloc_register(f"turned{b}") for b in range(2)]
            for b in range(2):
                pool.reg_mov(turned[b], 1)

            def unit(u):
                for t in range(TILES):
                    pool.wait_ge(s_idx[t], u * 16 + 16)
                    for g, vectors in enumerate(GROUPS):
                        b = (t * NG + g) % 2
                        if isinstance(u, int):
                            wait(pool, tp_full[b], (u - 1) * TU + (t * NG + g) // 2 + 1 if u else 0)
                        else:
                            pool.wait_ge(tp_full[b], turned[b])
                            pool.reg_add(turned[b], turned[b], 1)
                        for f in vectors:
                            if f:
                                nc.gpsimd.indirect_dma_start(
                                    emb[t][:, f, :], None, tables[f - 1],
                                    bass.IndirectOffsetOnAxis(ap=idx[t][:, f - 1:f], axis=0),
                                ).then_inc(s_emb[t][g], 16)

            units(pool, unit)

        def part(k):
            s = stage[staged_in(k)[0]]
            if k < NX:
                return s[0:VP, :], tab_hi[:, k, :, :], tab_lo[:, k, :, :]
            if k == NX:
                return s[0:ZP, :], wz_hi[:, 0:2, :], wz_lo[:, 0:2, :]
            if k == NX + 1:
                return s[0:ZP, 0:H1], wz_hi[:, 2, :], wz_lo[:, 2, :]
            if k == NX + 2:
                return s[:, :], w2_hi[:, :, :], w2_lo[:, :, :]
            return wd[:, :], wd_hi[:, :], wd_lo[:, :]

        def flat(ap):
            return ap if len(ap.shape) == 2 else ap.rearrange("p a b -> p (a b)")

        def embT_of(f, n, t):
            return embT[:, t, 0:P * F].rearrange("p (b f) -> p f b", f=F)[:, f:f + n, :]

        V_BANKS, Z_BANKS = [tp[0], tp[1], op, ip], [wp[0], tp[0], tp[1]]
        L1_BANKS, L2_BANKS, L3_BANK = [gp[0], gp[1], wp[1], op], [wp[0], ip], tp[0]

        def copy_pairs(copy, src, vectors):
            for i, f in enumerate(vectors):
                lot = slice(i % 2 * R, i % 2 * R + R)
                last = copy(pairs[:, :, OFF[f]:OFF[f] + F - 1 - f],
                            src[lot, i // 2 * P:(i // 2 + 1) * P].rearrange("p (j f) -> p j f", f=32)[:, :, f + 1:F])
            return last

        @block.vector
        def _(dve):
            def make_hot(v, k):
                n = v * NX + k
                wait(dve, op_full, n - 1)
                if isinstance(v, int) and v == 0:
                    dve.wait_ge(s_idx_hot[k // 2], 16)
                    for c in range(VC):
                        last = nc.vector.tensor_scalar(hot[k % 2][:, c, :], idx_hot[0:VP, k, :], row[0:VP, c:c + 1],
                                                       None, ALU.is_equal)
                    last.then_inc(hot_made, 1)
                    return
                if k % 2 == 0:
                    dve.wait_ge(ip_full, (v - 1) * NX // 2 + k // 2 + 1)
                indices = ip[0:VP, k % 2 * N:(k % 2 + 1) * N]
                nc.vector.tensor_tensor(hot[k % 2][:, :, :], indices.unsqueeze(1).broadcast_to([VP, VC, N]),
                                        row[0:VP, :].unsqueeze(2).broadcast_to([VP, VC, N]),
                                        ALU.is_equal).then_inc(hot_made, 1)

            def cut(k):
                src, hi, lo = part(k)
                if k == STAGED - 1:
                    place, come = staged_in(k)
                    dve.wait_ge(s_stage[place], come)
                    s = stage[place]
                    nc.vector.tensor_tensor(wd[:, :], s[:, 0:H1], s[:, H1:2 * H1], ALU.add).then_inc(s_wd, 1)
                dve.wait_ge(s_hi, k + 1)
                nc.vector.tensor_tensor(flat(lo), flat(src), flat(hi).bitcast(fp32), ALU.subtract).then_inc(s_lo, 1)

            dve.wait_ge(s_row, 1)
            make_hot(0, 0)
            make_hot(0, 1)
            cut(0)
            for k in range(1, NX):
                cut(k)
                if k + 1 < NX:
                    make_hot(0, k + 1)
            make_hot(1, 0)

            def unit(u):
                dve.wait_ge(op_free, (u + 1) * NX)
                if before(u, -1):
                    dve.wait_ge(gp_full[1], u * GU)
                for t in range(TILES):
                    nc.vector.tensor_copy(embT_of(NGV, NX, t), hotT[:, :, t * P:(t + 1) * P]).then_inc(hot_moved, 1)
                if not before(u, -1):
                    make_hot(1, 1)
                for step, a in steps(u):
                    if step == "D":
                        if before(u, -1):
                            dve.wait_ge(wp_full[L11 % 2], (u - 1) * WU + L11 // 2 + 1)
                        cut_dense(u)
                    elif step == "O" and before(u, 1):
                        if a + 2 < NX:
                            make_hot(u + 1, a + 2)
                        elif before(u, 2):
                            make_hot(u + 2, a + 2 - NX)
                    elif before(u, -1):
                        tower(u - 1, step, a)
                    elif step == "W":
                        cut(NX + a)

            def cut_dense(u):
                dve.wait_ge(tp_free[NG % 2], u * TU + NG // 2 + 1)
                src = denseT[:, :, :].rearrange("p j r -> p (j r)")
                nc.vector.tensor_copy(dense_hi[:, :], src).then_inc(dense_hi_done, 1)
                dve.wait_ge(dense_hi_done, u + 1)
                nc.vector.tensor_tensor(dense_lo[:, :], src, dense_hi[:, :].bitcast(fp32), ALU.subtract).then_inc(dense_cut, 1)

            def tower(u, step, a):
                if step == "Z":
                    for i, chunks in enumerate(Z_BATCHES):
                        b = (Z0 + i) % 2
                        cs = slice(chunks[0], chunks[-1] + 1)
                        dve.wait_ge(pairs_cut, u * 2 + i + 1)
                        nc.vector.tensor_tensor(flat(pairs_lo[:, cs, :]), wp[b][0:ZP, 0:len(chunks) * N],
                                                flat(pairs_hi[:, cs, :]).bitcast(fp32),
                                                ALU.subtract).then_inc(wp_free[b], 1)
                elif step == "L1":
                    dve.wait_ge(h1_cut, u * 2 + a + 1)
                    half = slice(2 * a, 2 * a + 2)
                    nc.vector.tensor_tensor(flat(h1_lo[:, half, :]), flat(h1[:, half, :]),
                                            flat(h1_hi[:, half, :]).bitcast(fp32), ALU.subtract).then_inc(h1_done, 1)

            def last_tower():
                for i in LAST_SHARE[1]:
                    dve.wait_ge(v_full, i + 1)
                    copy_pairs(nc.vector.tensor_copy, V_BANKS[i], LAST_V[i]).then_inc(v_dve, 1)
                for c in range(ZC):
                    dve.wait_ge(z_hi, c + 1)
                    nc.vector.tensor_tensor(pairs_lo[:, c, :], Z_BANKS[c][0:ZP, 0:N], pairs_hi[:, c, :].bitcast(fp32),
                                            ALU.subtract).then_inc(z_lo, 1)
                for m in range(M1):
                    dve.wait_ge(l1_raw, m + 1)
                    nc.vector.tensor_copy(h1_hi[:, m, :], h1[:, m, :]).then_inc(l1_hi, 1)
                    dve.wait_ge(l1_hi, m + 1)
                    nc.vector.tensor_tensor(h1_lo[:, m, :], h1[:, m, :], h1_hi[:, m, :].bitcast(fp32),
                                            ALU.subtract).then_inc(l1_lo, 1)
                dve.wait_ge(l2_full, 2)
                nc.vector.tensor_scalar(h2[:, 1, :], L2_BANKS[1][:, 0:N], b2[:, 1:2], 0.0, ALU.add, ALU.max).then_inc(h2_dve, 1)

            units(dve, unit)
            last_tower()

        @block.scalar
        def _(act):
            def copy(dst, src):
                return nc.scalar.activation(dst, src, ACT.Copy)

            def indices(v, k):
                n = v * NX + k
                if not (isinstance(v, int) and n == NX):
                    act.wait_ge(hot_made, n)
                act.wait_ge(s_idx_hot[k // 2], v * 16 + 16)
                copy(ip[0:VP, :], flat(idx_hot[0:VP, k:k + 2, :])).then_inc(ip_full, 1)

            def cut(k):
                src, hi, _ = part(k)
                if k < STAGED - 1:
                    place, come = staged_in(k)
                    act.wait_ge(s_stage[place], come)
                else:
                    act.wait_ge(s_wd, 1)
                copy(flat(hi), src).then_inc(s_hi, 1)

            def looked_up(v, k):
                n = v * NX + k
                act.wait_ge(op_full, n + 1)
                copy(hotT[:, k, :], op[:, 0:N]).then_inc(op_free, 1)

            def turned(u, t, part):
                for g in T_STEPS[part]:
                    vectors = GROUPS[g]
                    n = t * NG + g
                    b = n % 2
                    act.wait_ge(tp_full[b], u * TU + n // 2 + 1)
                    if g == 0:
                        if t == 0:
                            wait(act, dense_cut, u)
                        copy(denseT[:, :, t * Q:(t + 1) * Q],
                             tp[b][:, 0:P].rearrange("p (j q) -> p j q", q=Q))
                    copy(embT_of(vectors[0], len(vectors), t),
                         tp[b][:, 0:len(vectors) * P].rearrange("p (f b) -> p f b", b=P)
                         ).then_inc(tp_free[b], 1)

            for k in range(NX):
                cut(k)
                if k:
                    looked_up(0, k - 1)
                if k - 1 in T_FIRST:
                    turned(0, 0, T_FIRST.index(k - 1))
                if k == NX - 2:
                    indices(1, 0)
            looked_up(0, NX - 1)
            act.wait_ge(s_small, 48)

            def unit(u):
                for step, a in steps(u):
                    if step == "O" and a == 0:
                        act.wait_ge(hot_moved, (u + 1) * TILES)
                    if step == "T":
                        t, part = a
                        if t == 1:
                            turned(u, t, part)
                        elif before(u, 1):
                            turned(u + 1, t, part)
                    elif step == "G":
                        t, b = a
                        act.wait_ge(gp_full[b], u * GU + t + 1)
                        at = t * Q + b * QB
                        copy(gram[:, :, at:at + QB].rearrange("p f r -> p r f"),
                             gp[b][:, 0:QB * F].rearrange("p (q f) -> p q f", f=F)).then_inc(gp_free[b], 1)
                    elif step == "O":
                        if before(u, 1):
                            looked_up(u + 1, a)
                            if a % 2 == 0:
                                if a + 2 < NX:
                                    indices(u + 1, a + 2)
                                elif before(u, 2):
                                    indices(u + 2, 0)
                    elif before(u, -1):
                        tower(u - 1, step, a)
                    elif step == "W":
                        cut(NX + a)

            def tower(u, step, a):
                if step == "V":
                    for i in V_STEPS[a]:
                        b = i % 2
                        act.wait_ge(wp_full[b], u * WU + i // 2 + 1)
                        copy_pairs(copy, wp[b], VF[i]).then_inc(wp_free[b], 1)
                elif step == "Z":
                    for i, chunks in enumerate(Z_BATCHES):
                        n = Z0 + i
                        act.wait_ge(wp_full[n % 2], u * WU + n // 2 + 1)
                        copy(flat(pairs_hi[:, chunks[0]:chunks[-1] + 1, :]),
                             wp[n % 2][0:ZP, 0:len(chunks) * N]).then_inc(pairs_cut, 1)
                elif step == "L1":
                    n = L10 + a
                    act.wait_ge(wp_full[n % 2], u * WU + n // 2 + 1)
                    for i in range(2):
                        m = 2 * a + i
                        last = nc.scalar.activation(h1[:, m, :], wp[n % 2][:, i * N:(i + 1) * N], ACT.Relu, bias=b1[:, m:m + 1])
                        last.then_inc([h1_half, wp_free[n % 2]][i], 1)
                    act.wait_ge(h1_half, u * 2 + a + 1)
                    act.wait_ge(wp_free[n % 2], u * WU + n // 2 + 1)
                    half = slice(2 * a, 2 * a + 2)
                    copy(flat(h1_hi[:, half, :]), flat(h1[:, half, :])).then_inc(h1_cut, 1)
                elif step == "L2":
                    n = L20 + a
                    act.wait_ge(wp_full[n % 2], u * WU + n // 2 + 1)
                    nc.scalar.activation(h2[:, a, :], wp[n % 2][:, 0:N], ACT.Relu, bias=b2[:, a:a + 1]).then_inc(wp_free[n % 2], 1)
                elif step == "L3":
                    n = L30
                    act.wait_ge(wp_full[n % 2], u * WU + n // 2 + 1)
                    wait(act, s_out, u * 16)
                    copy(y[:, :], wp[n % 2][0:1, 0:N]).then_inc(wp_free[n % 2], 1)
                    act.wait_ge(wp_free[n % 2], u * WU + n // 2 + 1)
                    act.dma_start(out[bass.ds(u * N, N), :].rearrange("n o -> o n"), y[:, :]).then_inc(s_out, 16)

            def last_tower():
                for i in LAST_SHARE[0]:
                    act.wait_ge(v_full, i + 1)
                    copy_pairs(copy, V_BANKS[i], LAST_V[i]).then_inc(v_act, 1)
                for c in range(ZC):
                    act.wait_ge(z_full, c + 1)
                    copy(pairs_hi[:, c, :], Z_BANKS[c][0:ZP, 0:N]).then_inc(z_hi, 1)
                for m in range(M1):
                    act.wait_ge(l1_full, m + 1)
                    nc.scalar.activation(h1[:, m, :], L1_BANKS[m][:, 0:N], ACT.Relu,
                                         bias=b1[:, m:m + 1]).then_inc(l1_raw, 1)
                act.wait_ge(l2_full, 1)
                nc.scalar.activation(h2[:, 0, :], L2_BANKS[0][:, 0:N], ACT.Relu, bias=b2[:, 0:1]).then_inc(h2_act, 1)
                act.wait_ge(l3_full, 1)
                act.wait_ge(s_out, (U - 1) * 16)
                copy(y[:, :], L3_BANK[0:1, 0:N]).then_inc(y_done, 1)
                act.wait_ge(y_done, 1)
                act.dma_start(out[(U - 1) * N:U * N, :].rearrange("n o -> o n"), y[:, :]).then_inc(s_out, 16)

            act.wait_ge(s_lo, NX)
            units(act, unit)
            last_tower()
            act.wait_ge(s_out, U * 16)

        @block.tensor
        def _(pe):
            def look_up(v, k):
                n = v * NX + k
                pe.wait_ge(hot_made, n + 1)
                wait(pe, op_free, n)
                if isinstance(v, int) and v == 0:
                    pe.wait_ge(s_lo, k + 1)
                for c in range(VC):
                    for part_of in (tab_hi, tab_lo):
                        last = nc.tensor.matmul(op[:, 0:N], part_of[:, k, c, :], hot[k % 2][:, c, :],
                                                start=(c == 0 and part_of is tab_hi),
                                                stop=(c == VC - 1 and part_of is tab_lo))
                last.then_inc(op_full, 1)

            def products(o, terms):
                all_ = [m for w_hi, w_lo, x_hi, x_lo in terms for m in ((w_hi, x_hi), (w_hi, x_lo), (w_lo, x_hi))]
                for i, (w, x) in enumerate(all_):
                    last = nc.tensor.matmul(o, w, x, start=(i == 0), stop=(i == len(all_) - 1))
                return last

            def turn(u, t, part):
                for g in T_STEPS[part]:
                    vectors = GROUPS[g]
                    n = t * NG + g
                    b = n % 2
                    if g == 0:
                        pe.wait_ge(s_dense[t], u * 16 + 16)
                    rows = 16 * len([f for f in vectors if f])
                    pe.wait_ge(s_emb[t][g], u * rows + rows)
                    wait(pe, tp_free[b], u * TU + n // 2)
                    for i, f in enumerate(vectors):
                        last = nc.tensor.transpose(tp[b][:, i * P:(i + 1) * P], emb[t][:, f, :], ident[:, :])
                    last.then_inc(tp_full[b], 1)

            pe.wait_ge(s_ident, 1)
            pe.wait_ge(s_pad, 1)
            for k in range(NX):
                look_up(0, k)
                if k in T_FIRST:
                    turn(0, 0, T_FIRST.index(k))

            def unit(u):
                for step, a in steps(u):
                    if step == "T":
                        t, part = a
                        if t == 1:
                            turn(u, t, part)
                        elif before(u, 1):
                            turn(u + 1, t, part)
                    elif step == "G":
                        t, b = a
                        if b == 0:
                            for i in range(2):
                                pe.wait_ge(tp_free[i], u * TU + ((t + 1) * NG + 1 - i) // 2)
                            pe.wait_ge(hot_moved, u * TILES + t + 1)
                        wait(pe, gp_free[b], u * GU + t)
                        for j in range(J):
                            for q in range(QB):
                                at = (j * Q + b * QB + q) * F
                                last = nc.tensor.matmul(gp[b][32 * j:32 * j + 32, q * F:(q + 1) * F],
                                                        embT[:, t, at:at + 32], embT[:, t, at:at + F],
                                                        start=True, stop=True)
                        last.then_inc(gp_full[b], 1)
                    elif step == "O":
                        if before(u, 1):
                            look_up(u + 1, a)
                    elif before(u, -1):
                        tower(u - 1, step, a)

            turned = pe.alloc_register("turned")
            pe.reg_mov(turned, (Z0 + 1) // 2)

            def tower(u, step, a):
                if step == "V":
                    if a == 0:
                        for b in range(2):
                            pe.wait_ge(gp_free[b], (u + 1) * GU)
                    for i in V_STEPS[a]:
                        b = i % 2
                        wait(pe, wp_free[b], u * WU + i // 2)
                        for k, f in enumerate(VF[i][::2]):
                            last = nc.tensor.transpose(wp[b][:, k * P:(k + 1) * P],
                                                       gram[:, f:f + 2, :].rearrange("p f r -> p (f r)"), ident[:, :])
                        last.then_inc(wp_full[b], 1)
                elif step == "Z":
                    pe.wait_ge(wp_free[1], u * WU + Z0 // 2)
                    if isinstance(u, int):
                        pe.wait_ge(wp_free[0], u * WU + (Z0 + 1) // 2)
                    else:
                        pe.wait_ge(wp_free[0], turned)
                        pe.reg_add(turned, turned, WU)
                    for i, chunks in enumerate(Z_BATCHES):
                        b = (Z0 + i) % 2
                        for k, c in enumerate(chunks):
                            for j in range(J):
                                last = nc.tensor.transpose(wp[b][0:ZP, k * N + j * R:k * N + (j + 1) * R],
                                                           pairs[:, j, c * ZP:(c + 1) * ZP], ident[0:R, 0:R])
                        last.then_inc(wp_full[b], 1)
                elif step == "L1":
                    n = L10 + a
                    if a == 0:
                        pe.wait_ge(s_lo, STAGED)
                        for b in range(2):
                            pe.wait_ge(wp_free[b], u * WU + (L10 + 1 - b) // 2)
                        pe.wait_ge(dense_cut, u + 1)
                    wait(pe, wp_free[n % 2], u * WU + n // 2)
                    for i in range(2):
                        cols = slice((2 * a + i) * P, (2 * a + i + 1) * P)
                        last = products(wp[n % 2][:, i * N:(i + 1) * N],
                                        [(wd_hi[:, cols], wd_lo[:, cols], dense_hi[:, :], dense_lo[:, :])]
                                        + [(wz_hi[:, c, cols], wz_lo[:, c, cols], pairs_hi[:, c, :], pairs_lo[:, c, :])
                                           for c in range(ZC)])
                    last.then_inc(wp_full[n % 2], 1)
                elif step == "L2":
                    n = L20 + a
                    pe.wait_ge(h1_done, u * 2 + 2)
                    wait(pe, wp_free[n % 2], u * WU + n // 2)
                    cols = slice(a * P, (a + 1) * P)
                    products(wp[n % 2][:, 0:N], [(w2_hi[:, k, cols], w2_lo[:, k, cols], h1_hi[:, k, :], h1_lo[:, k, :])
                                                 for k in range(M1)]).then_inc(wp_full[n % 2], 1)
                elif step == "L3":
                    n = L30
                    for b in range(2):
                        pe.wait_ge(wp_free[b], u * WU + (L30 + 1 - b) // 2)
                    for k in range(M2):
                        last = nc.tensor.matmul(wp[n % 2][0:1, 0:N], w3[:, k:k + 1], h2[:, k, :],
                                                start=(k == 0), stop=(k == M2 - 1))
                    last.then_inc(wp_full[n % 2], 1)

            def last_tower():
                def layer_1(m, w_hi, w_lo, x_hi, x_lo, first=False, final=False):
                    cols = slice(m * P, (m + 1) * P)
                    o = L1_BANKS[m][:, 0:N]
                    nc.tensor.matmul(o, w_hi[:, cols], x_hi, start=first, stop=False)
                    nc.tensor.matmul(o, w_hi[:, cols], x_lo, start=False, stop=False)
                    return nc.tensor.matmul(o, w_lo[:, cols], x_hi, start=False, stop=final)

                def layer_1_dense(m):
                    layer_1(m, wd_hi, wd_lo, dense_hi[:, :], dense_lo[:, :], first=True)

                pe.wait_ge(dense_cut, U)
                for b in range(2):
                    pe.wait_ge(wp_free[b], (U - 1) * WU)
                pe.wait_ge(gp_free[0], U * GU)
                layer_1_dense(0)
                layer_1_dense(2)
                pe.wait_ge(gp_free[1], U * GU)
                for i, vectors in enumerate(LAST_V):
                    for k, f in enumerate(vectors[::2]):
                        last = nc.tensor.transpose(V_BANKS[i][:, k * P:(k + 1) * P],
                                                   gram[:, f:f + 2, :].rearrange("p f r -> p (f r)"), ident[:, :])
                    last.then_inc(v_full, 1)
                layer_1_dense(1)
                for c in range(ZC):
                    by_act, by_dve = LAST_Z_AFTER[c]
                    wait(pe, v_act, by_act)
                    wait(pe, v_dve, by_dve)
                    for j in range(J):
                        last = nc.tensor.transpose(Z_BANKS[c][0:ZP, j * R:(j + 1) * R],
                                                   pairs[:, j, c * ZP:(c + 1) * ZP], ident[0:R, 0:R])
                    last.then_inc(z_full, 1)
                layer_1_dense(3)
                for c in range(ZC):
                    pe.wait_ge(z_lo, c + 1)
                    for m in range(M1):
                        last = layer_1(m, wz_hi[:, c, :], wz_lo[:, c, :], pairs_hi[:, c, :], pairs_lo[:, c, :],
                                       final=c == ZC - 1)
                        if c == ZC - 1:
                            last.then_inc(l1_full, 1)
                for k in range(M1):
                    pe.wait_ge(l1_lo, k + 1)
                    for a in range(M2):
                        cols = slice(a * P, (a + 1) * P)
                        nc.tensor.matmul(L2_BANKS[a][:, 0:N], w2_hi[:, k, cols], h1_hi[:, k, :], start=(k == 0), stop=False)
                        nc.tensor.matmul(L2_BANKS[a][:, 0:N], w2_hi[:, k, cols], h1_lo[:, k, :], start=False, stop=False)
                        last = nc.tensor.matmul(L2_BANKS[a][:, 0:N], w2_lo[:, k, cols], h1_hi[:, k, :], start=False,
                                                stop=(k == M1 - 1))
                        if k == M1 - 1:
                            last.then_inc(l2_full, 1)
                pe.wait_ge(h2_act, 1)
                nc.tensor.matmul(L3_BANK[0:1, 0:N], w3[:, 0:1], h2[:, 0, :], start=True, stop=False)
                pe.wait_ge(h2_dve, 1)
                nc.tensor.matmul(L3_BANK[0:1, 0:N], w3[:, 1:2], h2[:, 1, :], start=False, stop=True).then_inc(l3_full, 1)

            units(pe, unit)
            last_tower()


def in_tiles(a):
    q = TILE // QUADS
    a = a.reshape(a.shape[0] // (TILE * TILES), QUADS, TILES, q, a.shape[1])
    return a.transpose(0, 2, 1, 3, 4).reshape(-1, a.shape[4])


def kernel(**inputs):
    import numpy as np
    import concourse.bacc as bacc
    from concourse.bass_utils import run_bass_kernel_spmd

    nc = bacc.Bacc("TRN2", target_bir_lowering=False, num_devices=1)
    arrays = {}

    def feed(name, a):
        a = np.ascontiguousarray(a)
        arrays[f"in_{name}"] = a
        return nc.dram_tensor(f"in_{name}", a.shape, mybir.dt.from_np(a.dtype), kind="ExternalInput").ap()

    n_tables = inputs["ids"].shape[1]
    by_size = sorted(range(n_tables), key=lambda i: inputs[f"tbl_{i}"].shape[0])
    one_hot = sorted(by_size[:ONE_HOT])
    gathered = [i for i in range(n_tables) if i not in one_hot]
    order = [0] + [i + 1 for i in gathered + one_hot]

    n_vectors, width = n_tables + 1, inputs["r_dense_output"].shape[1]
    row_of, row = {}, width
    for f in range(n_vectors):
        for g in range(f + 1, n_vectors):
            row_of[f, g] = row
            row += 1
    pair_rows = [row_of[min(order[a], order[b]), max(order[a], order[b])]
                 for a in range(n_vectors) for b in range(a + 1, n_vectors)]
    w_top1 = np.asarray(inputs["W_top1"])
    w_top1 = w_top1[list(range(width)) + pair_rows + list(range(row, w_top1.shape[0]))]

    ids_rows = in_tiles(np.asarray(inputs["ids"]))
    unit = TILE * TILES
    ids_hot = ids_rows[:, one_hot].reshape(-1, unit, ONE_HOT).transpose(0, 2, 1).reshape(-1, ONE_HOT * unit)
    by_partition = [np.asarray(inputs[n]).reshape(-1, TILE).T for n in ("b_top1", "b_top2", "W_top3")]

    dense = feed("dense", in_tiles(np.asarray(inputs["r_dense_output"])))
    ids = feed("ids", ids_rows[:, gathered])
    hot = feed("ids_hot", ids_hot)
    tables = [feed(f"tbl_{i}", np.asarray(inputs[f"tbl_{i}"])) for i in gathered]
    tables_hot = [feed(f"tbl_{i}", np.asarray(inputs[f"tbl_{i}"])) for i in one_hot]
    w1 = feed("W_top1", w_top1)
    w2 = feed("W_top2", np.asarray(inputs["W_top2"]))
    b1, b2, w3 = (feed(n, a) for n, a in zip(("b_top1", "b_top2", "W_top3"), by_partition))
    out = nc.dram_tensor("out_y", (dense.shape[0], 1), mybir.dt.float32, kind="ExternalOutput").ap()
    dlrm_tower_kernel(nc, dense, ids, hot, tables, tables_hot, w1, b1, w2, b2, w3, out)
    r = run_bass_kernel_spmd(nc, [arrays], core_ids=[0])
    return r.results[0]["out_y"]
```

```python
import concourse.bass as bass
from concourse import mybir
from contextlib import ExitStack

TILE, TILES, QUADS = 128, 2, 4
ONE_HOT = 8


def dlrm_tower_kernel(nc, dense, ids, ids_hot, tables, tables_hot, w_top1, b_top1, w_top2, b_top2, w_top3, out):
    fp32 = mybir.dt.float32
    fp32r = mybir.dt.float32r
    i32 = mybir.dt.int32
    ALU = mybir.AluOpType
    ACT = mybir.ActivationFunctionType

    P = 128
    D = dense.shape[1]
    B = dense.shape[0]
    NX = len(tables_hot)
    NGV = len(tables) + 1
    F = NGV + NX
    J, Q = QUADS, 32
    N = P * TILES
    R = TILES * Q
    U = B // N
    GROUPS = [range(g, min(g + 4, NGV)) for g in range(0, NGV, 4)]
    NG = len(GROUPS)
    QB = 16
    NP = F * (F - 1) // 2
    ZC = 3
    ZP = NP // ZC
    OFF = [f * (F - 1) - f * (f - 1) // 2 for f in range(F)]
    H1, H2 = w_top1.shape[1], w_top2.shape[1]
    M1, M2 = H1 // P, H2 // P
    V = tables_hot[0].shape[0]
    VC = 8
    VP = V // VC

    T_STEPS = [(0, 1), (2, 3), (4,)]
    ORDER = [("V", 0), ("T", (0, 2)), ("O", 0), ("V", 1), ("O", 1), ("V", 2), ("G", (0, 0)), ("C", (0, 0)), ("Z", 0), ("O", 2),
             ("G", (0, 1)), ("C", (0, 1)), ("T", (1, 0)), ("L1", 0), ("T", (1, 1)), ("O", 3), ("T", (1, 2)), ("L1", 1),
             ("O", 4), ("D", 0), ("G", (1, 0)), ("C", (1, 0)), ("L2", 0), ("O", 5), ("L2", 1), ("T", (0, 0)), ("O", 6),
             ("T", (0, 1)), ("G", (1, 1)), ("C", (1, 1)), ("O", 7), ("L3", 0)]
    FIRST = [("O", 0), ("G", (0, 0)), ("C", (0, 0)), ("W", 0), ("G", (0, 1)), ("C", (0, 1)), ("T", (1, 0)), ("O", 1),
             ("W", 1), ("T", (1, 1)), ("O", 2), ("W", 2), ("T", (1, 2)), ("O", 3), ("G", (1, 0)), ("C", (1, 0)), ("O", 4),
             ("W", 3), ("G", (1, 1)), ("C", (1, 1)), ("O", 5), ("D", 0), ("T", (0, 0)), ("O", 6), ("T", (0, 1)), ("O", 7)]
    LAST = [("T", (0, 2)), ("V", 0), ("G", (0, 0)), ("V", 1), ("V", 2), ("C", (0, 0)), ("G", (0, 1)), ("Z", 0),
            ("C", (0, 1)), ("T", (1, 0)), ("L1", 0), ("L1", 1), ("T", (1, 1)), ("D", 0), ("T", (1, 2)), ("L2", 0),
            ("G", (1, 0)), ("C", (1, 0)), ("L2", 1), ("G", (1, 1)), ("C", (1, 1)), ("L3", 0)]
    T_FIRST = [2, 5, 7]
    assert NX % 2 == 0 and NX == 8 and TILES * NG % 2 == 0 and NP % ZC == 0 and V == VC * VP
    assert M1 == 4 and M2 == 2 and U * N == B and U > 3

    VB = 3
    VF = [range(f, min(f + 2 * VB, F - 1)) for f in range(0, F - 1, 2 * VB)]
    assert F % 2 == 1
    V_STEPS = [(0, 1), (2, 3), (4,)]
    Z0 = len(VF)
    Z_BATCHES = [(0, 1), (2,)]
    L10 = Z0 + 2
    L11, L20 = L10 + 1, L10 + 2
    L30 = L20 + 2
    NB = L30 + 1
    LAST_V = [range(0, 6), range(6, 12), range(12, 18), range(18, F - 1)]
    LAST_SHARE = [(0, 2), (1, 3)]
    assert NB % 2 == 0 and Z0 == 5
    LAST_Z_AFTER = [(1, 0), (1, 1), (2, 2)]
    assert OFF[LAST_V[1][0]] >= ZP and OFF[LAST_V[2][0]] >= 2 * ZP

    ctx = ExitStack()
    with ctx:
        def sb_(name, shape, dt=fp32):
            return ctx.enter_context(nc.sbuf_tensor(name, shape, dt))

        def sem(name):
            return ctx.enter_context(nc.semaphore(name))

        idx = [sb_(f"idx{s}", [P, NGV - 1], i32) for s in range(2)]
        emb = [sb_(f"emb{s}", [P, NGV, D]) for s in range(2)]
        embT = sb_("embT", [P, TILES, P * F + 32 - F])
        hotT = sb_("hotT", [P, NX, N])
        idx_hot = sb_("idx_hot", [P, NX, N], i32)
        row_i = sb_("row_i", [P, VC], i32)
        less_row = sb_("less_row", [P, 1])
        row = sb_("row", [P, VC])
        hot = [sb_(f"hot{s}", [VP, VC, N], fp32r) for s in range(2)]
        tab_hi = sb_("tab_hi", [VP, NX, VC, D], fp32r)
        tab_lo = sb_("tab_lo", [VP, NX, VC, D], fp32r)
        denseT = sb_("denseT", [P, J, R])
        dense_hi = sb_("dense_hi", [P, N], fp32r)
        dense_lo = sb_("dense_lo", [P, N], fp32r)
        gram = sb_("gram", [P, F, R])
        pairs = sb_("pairs", [R, J, NP])
        pairs_hi = sb_("pairs_hi", [ZP, ZC, N], fp32r)
        pairs_lo = sb_("pairs_lo", [ZP, ZC, N], fp32r)
        h1 = sb_("h1", [P, M1, N])
        h1_hi = sb_("h1_hi", [P, M1, N], fp32r)
        h1_lo = sb_("h1_lo", [P, M1, N], fp32r)
        h2 = sb_("h2", [P, M2, N])
        S0 = NGV - VC
        stage = [h1[:, :, :].rearrange("p m n -> p (m n)"), gram[:, :, :].rearrange("p f r -> p (f r)")[:, 0:M1 * N],
                 embT[:, 1, NX * N:NX * N + VC * D], emb[1][:, S0:NGV, :].rearrange("p f d -> p (f d)"),
                 h2[:, :, :].rearrange("p m n -> p (m n)")]
        assert VC * D <= M1 * N <= F * R and NX * N + VC * D <= P * F and H1 <= M2 * N
        first_hot = embT[:, 1, 0:NX * N].rearrange("p (x n) -> p x n", n=N)
        y = sb_("y", [P, U * TILES])
        wz_hi = sb_("wz_hi", [ZP, ZC, H1], fp32r)
        wz_lo = sb_("wz_lo", [ZP, ZC, H1], fp32r)
        wd = sb_("wd", [P, H1])
        wd_hi = sb_("wd_hi", [P, H1], fp32r)
        wd_lo = sb_("wd_lo", [P, H1], fp32r)
        w2_hi = sb_("w2_hi", [P, M1, H2], fp32r)
        w2_lo = sb_("w2_lo", [P, M1, H2], fp32r)
        w3 = sb_("w3", [P, M2])
        b1 = sb_("b1", [P, M1])
        b2 = sb_("b2", [P, M2])
        ident = sb_("ident", [P, P])

        def bank(name):
            return ctx.enter_context(nc.psum_tensor(name, [P, 512], fp32))

        tp = [bank(f"tp{i}") for i in range(2)]
        op = bank("op")
        ip = bank("ip")
        gp = [bank(f"gp{i}") for i in range(2)]
        wp = [bank(f"wp{i}") for i in range(2)]

        s_ident = sem("s_ident")
        s_zero = sem("s_zero")
        s_pad = sem("s_pad")
        s_rowi = sem("s_rowi")
        s_less_row = sem("s_less_row")
        s_row = sem("s_row")
        s_stage = [sem(f"s_stage{s}") for s in range(5)]
        s_hi = sem("s_hi")
        s_lo = sem("s_lo")
        s_wd = sem("s_wd")
        s_small = sem("s_small")
        s_idx = [sem(f"s_idx{s}") for s in range(2)]
        s_dense = [sem(f"s_dense{s}") for s in range(2)]
        s_emb = [[sem(f"s_emb{s}_{g}") for g in range(NG)] for s in range(2)]
        s_idx_hot = [sem(f"s_idx_hot{i}") for i in range(NX // 2)]
        first_float = sem("first_float")
        ip_full = sem("ip_full")
        hot_made = sem("hot_made")
        op_full = sem("op_full")
        op_free = sem("op_free")
        hot_moved = sem("hot_moved")
        tp_full = [sem(f"tp_full{b}") for b in range(2)]
        tp_free = [sem(f"tp_free{b}") for b in range(2)]
        gp_full = [sem(f"gp_full{b}") for b in range(2)]
        gp_free = [sem(f"gp_free{b}") for b in range(2)]
        wp_full = [sem(f"wp_full{b}") for b in range(2)]
        wp_free = [sem(f"wp_free{b}") for b in range(2)]
        dense_hi_done = sem("dense_hi_done")
        h1_half = sem("h1_half")
        dense_cut = sem("dense_cut")
        pairs_cut = sem("pairs_cut")
        h1_cut = sem("h1_cut")
        h1_done = sem("h1_done")
        s_out = sem("s_out")
        v_full = sem("v_full")
        v_act = sem("v_act")
        v_dve = sem("v_dve")
        z_full = sem("z_full")
        z_hi = sem("z_hi")
        z_lo = sem("z_lo")
        l1_full = sem("l1_full")
        l1_raw = sem("l1_raw")
        l1_hi = sem("l1_hi")
        l1_lo = sem("l1_lo")
        l2_full = sem("l2_full")
        h2_act = sem("h2_act")
        h2_dve = sem("h2_dve")
        l3_full = sem("l3_full")
        y_done = sem("y_done")

        TU = TILES * NG // 2
        GU = TILES
        WU = NB // 2

        def wait(eng, semaphore, value):
            if not isinstance(value, int) or value > 0:
                eng.wait_ge(semaphore, value)

        def units(eng, unit):
            unit(0)
            with eng.Fori(1, U - 2) as u:
                unit(u)
            unit(U - 2)
            unit(U - 1)

        def before(u, a):
            return not isinstance(u, int) or 0 <= u + a < U

        def steps(u):
            return FIRST if not before(u, -1) else ORDER if before(u, 1) else LAST

        STAGED = NX + 4

        def staged_in(k):
            if k < NX:
                return k % 4, 16 * (k // 4 + 1), k - 3
            return [(0, 16 * (NX // 4 + 1), NX - 3), (4, 16, 0), (0, 16 * (NX // 4 + 2), NX + 1), (4, 48, NX + 2)][k - NX]

        block = ctx.enter_context(nc.Block())

        @block.sync
        def _(sp):
            def load_tile(u, t):
                at = u * N + t * P
                sp.dma_start(idx[t][:, :], ids[bass.ds(at, P), :]).then_inc(s_idx[t], 16)
                sp.dma_start(emb[t][:, 0, :], dense[bass.ds(at, P), :]).then_inc(s_dense[t], 16)

            def load_idx_hot(v, i):
                sp.dma_start(idx_hot[:, 2 * i:2 * i + 2, :],
                             ids_hot[bass.ds(v, 1), 2 * i * N:2 * (i + 1) * N].to_broadcast([P, 2 * N])
                             .rearrange("p (x n) -> p x n", n=N)).then_inc(s_idx_hot[i], 16)

            def load_stage(k):
                s, _, cut_before = staged_in(k)
                wait(sp, s_lo, cut_before)
                if k < NX:
                    sp.dma_start(stage[s][0:VP, :], tables_hot[k].rearrange("(p c) d -> p (c d)", c=VC)).then_inc(s_stage[s], 16)
                elif k == NX:
                    sp.dma_start(stage[s][0:ZP, :], w_top1[D:D + 2 * ZP, :].rearrange("(c p) n -> p c n", p=ZP)
                                 ).then_inc(s_stage[s], 16)
                elif k == NX + 1:
                    sp.dma_start(stage[s][0:ZP, 0:H1], w_top1[D + 2 * ZP:D + NP, :]).then_inc(s_stage[s], 16)
                elif k == NX + 2:
                    sp.dma_start(stage[s][:, :], w_top2.rearrange("(k p) n -> p k n", p=P)).then_inc(s_stage[s], 16)
                else:
                    sp.dma_start(wd[:, :], w_top1[0:D, :]).then_inc(s_stage[s], 16)
                    sp.dma_start(stage[s][:, 0:H1], w_top1[D + NP:, :]).then_inc(s_stage[s], 16)

            load_tile(0, 0)
            load_idx_hot(0, 0)
            load_stage(0)
            load_stage(1)
            load_idx_hot(0, 1)
            load_stage(2)
            load_stage(3)
            for i in range(2, NX // 2):
                load_idx_hot(0, i)
            load_tile(0, 1)
            for k in range(4, NX):
                load_stage(k)
            for i in range(NX // 2):
                sp.wait_ge(first_float, i + 1)
                load_idx_hot(1, i)
            sp.dma_start(w3[:, :], w_top3).then_inc(s_small, 16)
            sp.dma_start(b1[:, :], b_top1).then_inc(s_small, 16)
            sp.dma_start(b2[:, :], b_top2).then_inc(s_small, 16)
            load_stage(NX)
            load_stage(NX + 1)

            def unit(u):
                if before(u, 1):
                    for t in range(TILES):
                        n = (t + 1) * NG - 1
                        sp.wait_ge(tp_full[n % 2], u * TU + n // 2 + 1)
                        load_tile(u + 1, t)
                        if not before(u, -1) and t == 0:
                            load_stage(NX + 2)
                            load_stage(NX + 3)
                        if before(u, 2):
                            for i in (2 * t, 2 * t + 1):
                                sp.wait_ge(ip_full, u * NX // 2 + i + 1)
                                load_idx_hot(u + 2, i)

            units(sp, unit)

        @block.gpsimd
        def _(pool):
            nc.gpsimd.memset(ident[:, :], 0.0).then_inc(s_zero, 1)
            nc.gpsimd.iota(row_i[:, :], [[1, VC]], base=0, channel_multiplier=VC).then_inc(s_rowi, 1)
            nc.gpsimd.memset(embT[:, :, P * F:], 0.0).then_inc(s_pad, 1)
            pool.wait_ge(s_zero, 1)
            nc.gpsimd.affine_select(out=ident[:, :], in_=ident[:, :], compare_op=ALU.not_equal, fill=1.0,
                                    base=0, pattern=[[-1, P]], channel_multiplier=1).then_inc(s_ident, 1)
            pool.wait_ge(s_rowi, 1)
            nc.gpsimd.tensor_copy(row[:, :], row_i[:, :]).then_inc(s_row, 1)

            turned = [pool.alloc_register(f"turned{b}") for b in range(2)]
            for b in range(2):
                pool.reg_mov(turned[b], 1)

            def unit(u):
                for t in range(TILES):
                    pool.wait_ge(s_idx[t], u * 16 + 16)
                    for g, vectors in enumerate(GROUPS):
                        b = (t * NG + g) % 2
                        if isinstance(u, int):
                            wait(pool, tp_full[b], (u - 1) * TU + (t * NG + g) // 2 + 1 if u else 0)
                        else:
                            pool.wait_ge(tp_full[b], turned[b])
                            pool.reg_add(turned[b], turned[b], 1)
                        if not before(u, -1) and t == 1 and S0 in vectors:
                            pool.wait_ge(s_lo, NX)
                        for f in vectors:
                            if f:
                                nc.gpsimd.indirect_dma_start(
                                    emb[t][:, f, :], None, tables[f - 1],
                                    bass.IndirectOffsetOnAxis(ap=idx[t][:, f - 1:f], axis=0),
                                ).then_inc(s_emb[t][g], 16)

            units(pool, unit)

        def part(k):
            s = stage[staged_in(k)[0]]
            if k < NX:
                return s[0:VP, :], tab_hi[:, k, :, :], tab_lo[:, k, :, :]
            if k == NX:
                return s[0:ZP, :], wz_hi[:, 0:2, :], wz_lo[:, 0:2, :]
            if k == NX + 1:
                return s[0:ZP, 0:H1], wz_hi[:, 2, :], wz_lo[:, 2, :]
            if k == NX + 2:
                return s[:, :], w2_hi[:, :, :], w2_lo[:, :, :]
            return wd[:, :], wd_hi[:, :], wd_lo[:, :]

        def flat(ap):
            return ap if len(ap.shape) == 2 else ap.rearrange("p a b -> p (a b)")

        def embT_of(f, n, t):
            return embT[:, t, 0:P * F].rearrange("p (b f) -> p f b", f=F)[:, f:f + n, :]

        def o_bank(v, k):
            return wp[0] if isinstance(v, int) and v == 0 and k % 2 else op

        V_BANKS, Z_BANKS = [tp[0], tp[1], op, ip], [wp[0], tp[0], tp[1]]
        L1_BANKS, L2_BANKS, L3_BANK = [gp[0], gp[1], wp[1], op], [wp[0], ip], tp[0]

        def copy_pairs(copy, src, vectors):
            for i, f in enumerate(vectors):
                lot = slice(i % 2 * R, i % 2 * R + R)
                last = copy(pairs[:, :, OFF[f]:OFF[f] + F - 1 - f],
                            src[lot, i // 2 * P:(i // 2 + 1) * P].rearrange("p (j f) -> p j f", f=32)[:, :, f + 1:F])
            return last

        @block.vector
        def _(dve):
            def make_hot(v, k):
                n = v * NX + k
                wait(dve, op_full, n - 1)
                if isinstance(v, int) and v == 0:
                    dve.wait_ge(first_float, k // 2 + 1)
                    for c in range(VC):
                        last = nc.vector.tensor_scalar(hot[k % 2][:, c, :], first_hot[0:VP, k, :], float(c),
                                                       None, ALU.is_equal)
                    last.then_inc(hot_made, 1)
                    return
                if k % 2 == 0:
                    dve.wait_ge(ip_full, (v - 1) * NX // 2 + k // 2 + 1)
                indices = ip[0:VP, k % 2 * N:(k % 2 + 1) * N]
                nc.vector.tensor_tensor(hot[k % 2][:, :, :], indices.unsqueeze(1).broadcast_to([VP, VC, N]),
                                        row[0:VP, :].unsqueeze(2).broadcast_to([VP, VC, N]),
                                        ALU.is_equal).then_inc(hot_made, 1)

            def cut(k):
                src, hi, lo = part(k)
                if k == STAGED - 1:
                    place, come, _ = staged_in(k)
                    dve.wait_ge(s_stage[place], come)
                    nc.vector.tensor_tensor(wd[:, :], wd[:, :], stage[place][:, 0:H1], ALU.add).then_inc(s_wd, 1)
                dve.wait_ge(s_hi, k + 1)
                nc.vector.tensor_tensor(flat(lo), flat(src), flat(hi).bitcast(fp32), ALU.subtract).then_inc(s_lo, 1)

            dve.wait_ge(s_row, 1)
            make_hot(0, 0)
            cut(0)
            make_hot(0, 1)
            cut(1)
            for k in range(2, NX):
                cut(k)
                make_hot(0, k)
            make_hot(1, 0)

            def unit(u):
                dve.wait_ge(op_free, (u + 1) * NX)
                if before(u, -1):
                    dve.wait_ge(gp_full[1], u * GU)
                for t in range(TILES):
                    nc.vector.tensor_copy(embT_of(NGV, NX, t), hotT[:, :, t * P:(t + 1) * P]).then_inc(hot_moved, 1)
                if not before(u, -1):
                    make_hot(1, 1)
                for step, a in steps(u):
                    if step == "D":
                        if before(u, -1):
                            dve.wait_ge(wp_full[L11 % 2], (u - 1) * WU + L11 // 2 + 1)
                        cut_dense(u)
                    elif step == "O" and before(u, 1):
                        if a + 2 < NX:
                            make_hot(u + 1, a + 2)
                        elif before(u, 2):
                            make_hot(u + 2, a + 2 - NX)
                    elif before(u, -1):
                        tower(u - 1, step, a)
                    elif step == "W":
                        cut(NX + a)

            def cut_dense(u):
                dve.wait_ge(tp_free[NG % 2], u * TU + NG // 2 + 1)
                src = denseT[:, :, :].rearrange("p j r -> p (j r)")
                nc.vector.tensor_copy(dense_hi[:, :], src).then_inc(dense_hi_done, 1)
                dve.wait_ge(dense_hi_done, u + 1)
                nc.vector.tensor_tensor(dense_lo[:, :], src, dense_hi[:, :].bitcast(fp32), ALU.subtract).then_inc(dense_cut, 1)

            def tower(u, step, a):
                if step == "Z":
                    for i, chunks in enumerate(Z_BATCHES):
                        b = (Z0 + i) % 2
                        cs = slice(chunks[0], chunks[-1] + 1)
                        dve.wait_ge(pairs_cut, u * 2 + i + 1)
                        nc.vector.tensor_tensor(flat(pairs_lo[:, cs, :]), wp[b][0:ZP, 0:len(chunks) * N],
                                                flat(pairs_hi[:, cs, :]).bitcast(fp32),
                                                ALU.subtract).then_inc(wp_free[b], 1)
                elif step == "L1":
                    dve.wait_ge(h1_cut, u * 2 + a + 1)
                    half = slice(2 * a, 2 * a + 2)
                    nc.vector.tensor_tensor(flat(h1_lo[:, half, :]), flat(h1[:, half, :]),
                                            flat(h1_hi[:, half, :]).bitcast(fp32), ALU.subtract).then_inc(h1_done, 1)

            def last_tower():
                for i in LAST_SHARE[1]:
                    dve.wait_ge(v_full, i + 1)
                    copy_pairs(nc.vector.tensor_copy, V_BANKS[i], LAST_V[i]).then_inc(v_dve, 1)
                for c in range(ZC):
                    dve.wait_ge(z_hi, c + 1)
                    nc.vector.tensor_tensor(pairs_lo[:, c, :], Z_BANKS[c][0:ZP, 0:N], pairs_hi[:, c, :].bitcast(fp32),
                                            ALU.subtract).then_inc(z_lo, 1)
                for m in range(M1):
                    dve.wait_ge(l1_raw, m + 1)
                    nc.vector.tensor_copy(h1_hi[:, m, :], h1[:, m, :]).then_inc(l1_hi, 1)
                    dve.wait_ge(l1_hi, m + 1)
                    nc.vector.tensor_tensor(h1_lo[:, m, :], h1[:, m, :], h1_hi[:, m, :].bitcast(fp32),
                                            ALU.subtract).then_inc(l1_lo, 1)
                dve.wait_ge(l2_full, 2)
                nc.vector.tensor_scalar(h2[:, 1, :], L2_BANKS[1][:, 0:N], b2[:, 1:2], 0.0, ALU.add, ALU.max).then_inc(h2_dve, 1)

            units(dve, unit)
            last_tower()

        @block.scalar
        def _(act):
            def copy(dst, src):
                return nc.scalar.activation(dst, src, ACT.Copy)

            def indices(v, k):
                n = v * NX + k
                if not (isinstance(v, int) and n == NX):
                    act.wait_ge(hot_made, n)
                act.wait_ge(s_idx_hot[k // 2], v * 16 + 16)
                copy(ip[0:VP, :], flat(idx_hot[0:VP, k:k + 2, :])).then_inc(ip_full, 1)

            def cut(k):
                src, hi, _ = part(k)
                if k < STAGED - 1:
                    place, come, _ = staged_in(k)
                    act.wait_ge(s_stage[place], come)
                else:
                    act.wait_ge(s_wd, 1)
                copy(flat(hi), src).then_inc(s_hi, 1)

            def looked_up(v, k):
                n = v * NX + k
                act.wait_ge(op_full, n + 1)
                copy(hotT[:, k, :], o_bank(v, k)[:, 0:N]).then_inc(op_free, 1)

            def turned(u, t, part):
                for g in T_STEPS[part]:
                    vectors = GROUPS[g]
                    n = t * NG + g
                    b = n % 2
                    act.wait_ge(tp_full[b], u * TU + n // 2 + 1)
                    if g == 0:
                        if t == 0:
                            wait(act, dense_cut, u)
                        copy(denseT[:, :, t * Q:(t + 1) * Q],
                             tp[b][:, 0:P].rearrange("p (j q) -> p j q", q=Q))
                    copy(embT_of(vectors[0], len(vectors), t),
                         tp[b][:, 0:len(vectors) * P].rearrange("p (f b) -> p f b", b=P)
                         ).then_inc(tp_free[b], 1)

            def first_indices(i):
                act.wait_ge(s_idx_hot[i], 16)
                nc.scalar.activation(first_hot[0:VP, 2 * i:2 * i + 2, :], idx_hot[0:VP, 2 * i:2 * i + 2, :], ACT.Identity,
                                     bias=less_row[0:VP, :]).then_inc(first_float, 1)

            act.wait_ge(s_rowi, 1)
            nc.scalar.activation(less_row[:, :], row_i[:, 0:1], ACT.Identity, scale=-1.0).then_inc(s_less_row, 1)
            act.wait_ge(s_less_row, 1)
            first_indices(0)
            for k in range(NX + 2):
                if k < NX:
                    cut(k)
                if k % 2 == 0 and k + 2 < NX:
                    first_indices(k // 2 + 1)
                if k >= 2:
                    looked_up(0, k - 2)
                    if k - 2 in T_FIRST:
                        turned(0, 0, T_FIRST.index(k - 2))
                if k == NX - 2:
                    indices(1, 0)
            act.wait_ge(s_small, 48)

            def unit(u):
                for step, a in steps(u):
                    if step == "O" and a == 0:
                        act.wait_ge(hot_moved, (u + 1) * TILES)
                    if step == "T":
                        t, part = a
                        if t == 1 or part == 2:
                            turned(u, t, part)
                        elif before(u, 1):
                            turned(u + 1, t, part)
                    elif step == "C":
                        t, b = a
                        act.wait_ge(gp_full[b], u * GU + t + 1)
                        at = t * Q + b * QB
                        copy(gram[:, :, at:at + QB].rearrange("p f r -> p r f"),
                             gp[b][:, 0:QB * F].rearrange("p (q f) -> p q f", f=F)).then_inc(gp_free[b], 1)
                    elif step == "O":
                        if before(u, 1):
                            looked_up(u + 1, a)
                            if a % 2 == 0:
                                if a + 2 < NX:
                                    indices(u + 1, a + 2)
                                elif before(u, 2):
                                    indices(u + 2, 0)
                    elif before(u, -1):
                        tower(u - 1, step, a)
                    elif step == "W":
                        cut(NX + a)

            def tower(u, step, a):
                if step == "V":
                    for i in V_STEPS[a]:
                        b = i % 2
                        act.wait_ge(wp_full[b], u * WU + i // 2 + 1)
                        copy_pairs(copy, wp[b], VF[i]).then_inc(wp_free[b], 1)
                elif step == "Z":
                    for i, chunks in enumerate(Z_BATCHES):
                        n = Z0 + i
                        act.wait_ge(wp_full[n % 2], u * WU + n // 2 + 1)
                        copy(flat(pairs_hi[:, chunks[0]:chunks[-1] + 1, :]),
                             wp[n % 2][0:ZP, 0:len(chunks) * N]).then_inc(pairs_cut, 1)
                elif step == "L1":
                    n = L10 + a
                    act.wait_ge(wp_full[n % 2], u * WU + n // 2 + 1)
                    for i in range(2):
                        m = 2 * a + i
                        last = nc.scalar.activation(h1[:, m, :], wp[n % 2][:, i * N:(i + 1) * N], ACT.Relu, bias=b1[:, m:m + 1])
                        last.then_inc([h1_half, wp_free[n % 2]][i], 1)
                    act.wait_ge(h1_half, u * 2 + a + 1)
                    act.wait_ge(wp_free[n % 2], u * WU + n // 2 + 1)
                    half = slice(2 * a, 2 * a + 2)
                    copy(flat(h1_hi[:, half, :]), flat(h1[:, half, :])).then_inc(h1_cut, 1)
                elif step == "L2":
                    n = L20 + a
                    act.wait_ge(wp_full[n % 2], u * WU + n // 2 + 1)
                    nc.scalar.activation(h2[:, a, :], wp[n % 2][:, 0:N], ACT.Relu, bias=b2[:, a:a + 1]).then_inc(wp_free[n % 2], 1)
                elif step == "L3":
                    n = L30
                    act.wait_ge(wp_full[n % 2], u * WU + n // 2 + 1)
                    copy(y[:, bass.ds(u * TILES, TILES)], wp[n % 2][:, 0:TILES]).then_inc(wp_free[n % 2], 1)

            def last_tower():
                for i in LAST_SHARE[0]:
                    act.wait_ge(v_full, i + 1)
                    copy_pairs(copy, V_BANKS[i], LAST_V[i]).then_inc(v_act, 1)
                for c in range(ZC):
                    act.wait_ge(z_full, c + 1)
                    copy(pairs_hi[:, c, :], Z_BANKS[c][0:ZP, 0:N]).then_inc(z_hi, 1)
                for m in range(M1):
                    act.wait_ge(l1_full, m + 1)
                    nc.scalar.activation(h1[:, m, :], L1_BANKS[m][:, 0:N], ACT.Relu,
                                         bias=b1[:, m:m + 1]).then_inc(l1_raw, 1)
                act.wait_ge(l2_full, 1)
                nc.scalar.activation(h2[:, 0, :], L2_BANKS[0][:, 0:N], ACT.Relu, bias=b2[:, 0:1]).then_inc(h2_act, 1)
                act.wait_ge(l3_full, 1)
                copy(y[:, (U - 1) * TILES:U * TILES], L3_BANK[:, 0:TILES]).then_inc(y_done, 1)
                act.wait_ge(y_done, 1)
                act.wait_ge(wp_free[L30 % 2], (U - 1) * WU)
                act.dma_start(out, y[:, :]).then_inc(s_out, 16)

            act.wait_ge(s_lo, NX)
            units(act, unit)
            last_tower()
            act.wait_ge(s_out, 16)

        @block.tensor
        def _(pe):
            def look_up(v, k):
                n = v * NX + k
                pe.wait_ge(hot_made, n + 1)
                first = isinstance(v, int) and v == 0
                wait(pe, op_free, n - 1 if first else n)
                if first:
                    pe.wait_ge(s_lo, k + 1)
                for c in range(VC):
                    for part_of in (tab_hi, tab_lo):
                        last = nc.tensor.matmul(o_bank(v, k)[:, 0:N], part_of[:, k, c, :], hot[k % 2][:, c, :],
                                                start=(c == 0 and part_of is tab_hi),
                                                stop=(c == VC - 1 and part_of is tab_lo))
                last.then_inc(op_full, 1)

            def products(o, terms):
                all_ = [m for w_hi, w_lo, x_hi, x_lo in terms for m in ((w_hi, x_hi), (w_hi, x_lo), (w_lo, x_hi))]
                for i, (w, x) in enumerate(all_):
                    last = nc.tensor.matmul(o, w, x, start=(i == 0), stop=(i == len(all_) - 1))
                return last

            def turn(u, t, part):
                for g in T_STEPS[part]:
                    vectors = GROUPS[g]
                    n = t * NG + g
                    b = n % 2
                    if g == 0:
                        pe.wait_ge(s_dense[t], u * 16 + 16)
                    rows = 16 * len([f for f in vectors if f])
                    pe.wait_ge(s_emb[t][g], u * rows + rows)
                    wait(pe, tp_free[b], u * TU + n // 2)
                    for i, f in enumerate(vectors):
                        last = nc.tensor.transpose(tp[b][:, i * P:(i + 1) * P], emb[t][:, f, :], ident[:, :])
                    last.then_inc(tp_full[b], 1)

            pe.wait_ge(s_ident, 1)
            pe.wait_ge(s_pad, 1)
            for k in range(NX):
                look_up(0, k)
                if k in T_FIRST:
                    turn(0, 0, T_FIRST.index(k))

            def unit(u):
                for step, a in steps(u):
                    if step == "T":
                        t, part = a
                        if t == 1 or part == 2:
                            turn(u, t, part)
                        elif before(u, 1):
                            turn(u + 1, t, part)
                    elif step == "G":
                        t, b = a
                        if b == 0:
                            for i in range(2):
                                pe.wait_ge(tp_free[i], u * TU + ((t + 1) * NG + 1 - i) // 2)
                            pe.wait_ge(hot_moved, u * TILES + t + 1)
                        wait(pe, gp_free[b], u * GU + t)
                        for q in range(QB):
                            for j in range(J):
                                at = (j * Q + b * QB + q) * F
                                last = nc.tensor.matmul(gp[b][32 * j:32 * j + 32, q * F:(q + 1) * F],
                                                        embT[:, t, at:at + 32], embT[:, t, at:at + F],
                                                        start=True, stop=True)
                        last.then_inc(gp_full[b], 1)
                    elif step == "O":
                        if before(u, 1):
                            look_up(u + 1, a)
                    elif before(u, -1):
                        tower(u - 1, step, a)

            turned = pe.alloc_register("turned")
            pe.reg_mov(turned, (Z0 + 1) // 2)

            def tower(u, step, a):
                if step == "V":
                    if a == 0:
                        for b in range(2):
                            pe.wait_ge(gp_free[b], (u + 1) * GU)
                    for i in V_STEPS[a]:
                        b = i % 2
                        wait(pe, wp_free[b], u * WU + i // 2)
                        for k, f in enumerate(VF[i][::2]):
                            last = nc.tensor.transpose(wp[b][:, k * P:(k + 1) * P],
                                                       gram[:, f:f + 2, :].rearrange("p f r -> p (f r)"), ident[:, :])
                        last.then_inc(wp_full[b], 1)
                elif step == "Z":
                    pe.wait_ge(wp_free[1], u * WU + Z0 // 2)
                    if isinstance(u, int):
                        pe.wait_ge(wp_free[0], u * WU + (Z0 + 1) // 2)
                    else:
                        pe.wait_ge(wp_free[0], turned)
                        pe.reg_add(turned, turned, WU)
                    for i, chunks in enumerate(Z_BATCHES):
                        b = (Z0 + i) % 2
                        for k, c in enumerate(chunks):
                            for j in range(J):
                                last = nc.tensor.transpose(wp[b][0:ZP, k * N + j * R:k * N + (j + 1) * R],
                                                           pairs[:, j, c * ZP:(c + 1) * ZP], ident[0:R, 0:R])
                        last.then_inc(wp_full[b], 1)
                elif step == "L1":
                    n = L10 + a
                    if a == 0:
                        pe.wait_ge(s_lo, STAGED)
                        for b in range(2):
                            pe.wait_ge(wp_free[b], u * WU + (L10 + 1 - b) // 2)
                        pe.wait_ge(dense_cut, u + 1)
                    wait(pe, wp_free[n % 2], u * WU + n // 2)
                    for i in range(2):
                        cols = slice((2 * a + i) * P, (2 * a + i + 1) * P)
                        last = products(wp[n % 2][:, i * N:(i + 1) * N],
                                        [(wd_hi[:, cols], wd_lo[:, cols], dense_hi[:, :], dense_lo[:, :])]
                                        + [(wz_hi[:, c, cols], wz_lo[:, c, cols], pairs_hi[:, c, :], pairs_lo[:, c, :])
                                           for c in range(ZC)])
                    last.then_inc(wp_full[n % 2], 1)
                elif step == "L2":
                    n = L20 + a
                    pe.wait_ge(h1_done, u * 2 + 2)
                    wait(pe, wp_free[n % 2], u * WU + n // 2)
                    cols = slice(a * P, (a + 1) * P)
                    products(wp[n % 2][:, 0:N], [(w2_hi[:, k, cols], w2_lo[:, k, cols], h1_hi[:, k, :], h1_lo[:, k, :])
                                                 for k in range(M1)]).then_inc(wp_full[n % 2], 1)
                elif step == "L3":
                    n = L30
                    for b in range(2):
                        pe.wait_ge(wp_free[b], u * WU + (L30 + 1 - b) // 2)
                    for i in range(TILES):
                        for k in range(M2):
                            last = nc.tensor.matmul(wp[n % 2][:, i:i + 1], h2[:, k, i * P:(i + 1) * P], w3[:, k:k + 1],
                                                    start=(k == 0), stop=(k == M2 - 1))
                    last.then_inc(wp_full[n % 2], 1)

            def last_tower():
                def layer_1(m, w_hi, w_lo, x_hi, x_lo, first=False, final=False):
                    cols = slice(m * P, (m + 1) * P)
                    o = L1_BANKS[m][:, 0:N]
                    nc.tensor.matmul(o, w_hi[:, cols], x_hi, start=first, stop=False)
                    nc.tensor.matmul(o, w_hi[:, cols], x_lo, start=False, stop=False)
                    return nc.tensor.matmul(o, w_lo[:, cols], x_hi, start=False, stop=final)

                def layer_1_dense(m):
                    layer_1(m, wd_hi, wd_lo, dense_hi[:, :], dense_lo[:, :], first=True)

                pe.wait_ge(dense_cut, U)
                for b in range(2):
                    pe.wait_ge(wp_free[b], (U - 1) * WU)
                pe.wait_ge(gp_free[0], U * GU)
                layer_1_dense(0)
                layer_1_dense(2)
                pe.wait_ge(gp_free[1], U * GU)
                for i, vectors in enumerate(LAST_V):
                    for k, f in enumerate(vectors[::2]):
                        last = nc.tensor.transpose(V_BANKS[i][:, k * P:(k + 1) * P],
                                                   gram[:, f:f + 2, :].rearrange("p f r -> p (f r)"), ident[:, :])
                    last.then_inc(v_full, 1)
                layer_1_dense(1)
                for c in range(ZC):
                    by_act, by_dve = LAST_Z_AFTER[c]
                    wait(pe, v_act, by_act)
                    wait(pe, v_dve, by_dve)
                    for j in range(J):
                        last = nc.tensor.transpose(Z_BANKS[c][0:ZP, j * R:(j + 1) * R],
                                                   pairs[:, j, c * ZP:(c + 1) * ZP], ident[0:R, 0:R])
                    last.then_inc(z_full, 1)
                layer_1_dense(3)
                for c in range(ZC):
                    pe.wait_ge(z_lo, c + 1)
                    for m in range(M1):
                        last = layer_1(m, wz_hi[:, c, :], wz_lo[:, c, :], pairs_hi[:, c, :], pairs_lo[:, c, :],
                                       final=c == ZC - 1)
                        if c == ZC - 1:
                            last.then_inc(l1_full, 1)
                for k in range(M1):
                    pe.wait_ge(l1_lo, k + 1)
                    for a in range(M2):
                        cols = slice(a * P, (a + 1) * P)
                        nc.tensor.matmul(L2_BANKS[a][:, 0:N], w2_hi[:, k, cols], h1_hi[:, k, :], start=(k == 0), stop=False)
                        nc.tensor.matmul(L2_BANKS[a][:, 0:N], w2_hi[:, k, cols], h1_lo[:, k, :], start=False, stop=False)
                        last = nc.tensor.matmul(L2_BANKS[a][:, 0:N], w2_lo[:, k, cols], h1_hi[:, k, :], start=False,
                                                stop=(k == M1 - 1))
                        if k == M1 - 1:
                            last.then_inc(l2_full, 1)
                pe.wait_ge(h2_act, 1)
                pe.wait_ge(h2_dve, 1)
                for i in range(TILES):
                    for k in range(M2):
                        last = nc.tensor.matmul(L3_BANK[:, i:i + 1], h2[:, k, i * P:(i + 1) * P], w3[:, k:k + 1],
                                                start=(k == 0), stop=(k == M2 - 1))
                last.then_inc(l3_full, 1)

            units(pe, unit)
            last_tower()


def in_tiles(a):
    q = TILE // QUADS
    a = a.reshape(a.shape[0] // (TILE * TILES), QUADS, TILES, q, a.shape[1])
    return a.transpose(0, 2, 1, 3, 4).reshape(-1, a.shape[4])


def kernel(**inputs):
    import numpy as np
    import concourse.bacc as bacc
    from concourse.bass_utils import run_bass_kernel_spmd

    nc = bacc.Bacc("TRN2", target_bir_lowering=False, num_devices=1)
    arrays = {}

    def feed(name, a):
        a = np.ascontiguousarray(a)
        arrays[f"in_{name}"] = a
        return nc.dram_tensor(f"in_{name}", a.shape, mybir.dt.from_np(a.dtype), kind="ExternalInput").ap()

    n_tables = inputs["ids"].shape[1]
    by_size = sorted(range(n_tables), key=lambda i: inputs[f"tbl_{i}"].shape[0])
    one_hot = sorted(by_size[:ONE_HOT])
    gathered = [i for i in range(n_tables) if i not in one_hot]
    order = [0] + [i + 1 for i in gathered + one_hot]

    n_vectors, width = n_tables + 1, inputs["r_dense_output"].shape[1]
    row_of, row = {}, width
    for f in range(n_vectors):
        for g in range(f + 1, n_vectors):
            row_of[f, g] = row
            row += 1
    pair_rows = [row_of[min(order[a], order[b]), max(order[a], order[b])]
                 for a in range(n_vectors) for b in range(a + 1, n_vectors)]
    w_top1 = np.asarray(inputs["W_top1"])
    w_top1 = w_top1[list(range(width)) + pair_rows + list(range(row, w_top1.shape[0]))]

    ids_rows = in_tiles(np.asarray(inputs["ids"]))
    unit = TILE * TILES
    ids_hot = ids_rows[:, one_hot].reshape(-1, unit, ONE_HOT).transpose(0, 2, 1).reshape(-1, ONE_HOT * unit)
    by_partition = [np.asarray(inputs[n]).reshape(-1, TILE).T for n in ("b_top1", "b_top2", "W_top3")]

    dense = feed("dense", in_tiles(np.asarray(inputs["r_dense_output"])))
    ids = feed("ids", ids_rows[:, gathered])
    hot = feed("ids_hot", ids_hot)
    tables = [feed(f"tbl_{i}", np.asarray(inputs[f"tbl_{i}"])) for i in gathered]
    tables_hot = [feed(f"tbl_{i}", np.asarray(inputs[f"tbl_{i}"])) for i in one_hot]
    w1 = feed("W_top1", w_top1)
    w2 = feed("W_top2", np.asarray(inputs["W_top2"]))
    b1, b2, w3 = (feed(n, a) for n, a in zip(("b_top1", "b_top2", "W_top3"), by_partition))
    out = nc.dram_tensor("out_y", (TILE, dense.shape[0] // TILE), mybir.dt.float32, kind="ExternalOutput").ap()
    dlrm_tower_kernel(nc, dense, ids, hot, tables, tables_hot, w1, b1, w2, b2, w3, out)
    r = run_bass_kernel_spmd(nc, [arrays], core_ids=[0])
    return np.ascontiguousarray(r.results[0]["out_y"].T).reshape(-1, 1)
```
